# Optimizing a Trainium2 kernel written in Bass

```python
import numpy as np
import jax
import jax.numpy as jnp

def _softmax(x, axis=-1):
    return jax.nn.softmax(x, axis=axis)

def _gelu(x):
    return jax.nn.gelu(x, approximate=True)

def _silu(x):
    return jax.nn.silu(x)

def _sigmoid(x):
    return jax.nn.sigmoid(x)

def _layernorm(x, axis=-1, eps=1e-05):
    m = jnp.mean(x, axis=axis, keepdims=True)
    v = jnp.var(x, axis=axis, keepdims=True)
    return (x - m) / jnp.sqrt(v + eps)

def _scatter_add(tgt, idx, src, axis=0):
    return tgt.at[idx].add(src)

def _segment_sum(src, seg, n):
    return jax.ops.segment_sum(src, seg, n)
kernel_name = 'mk_gnn_preln_d1_gnn_r8_b54f7f'

def setup_inputs(seed: int=0):
    np.random.seed(seed)
    _w = jnp.asarray

    def _rec_inputs():
        import jax
        import jax.numpy as jnp
        _gk = jax.random.key(seed)
        x = -0.000202 + 1 * jax.random.normal(jax.random.fold_in(_gk, 1), (12500, 64), jnp.float32)
        _s = jax.random.randint(jax.random.fold_in(_gk, 2), (100000,), 0, 12500, jnp.int32)
        _d = jax.random.randint(jax.random.fold_in(_gk, 3), (100000,), 0, 12500, jnp.int32)
        _loop = jnp.arange(12500, dtype=jnp.int32)
        src = jnp.concatenate([_s, _d, _loop])
        dst = jnp.concatenate([_d, _s, _loop])
        _o = jnp.argsort(dst, stable=True)
        src = src[_o]
        dst = dst[_o]
        edge_attr_64 = -8.16379e-05 + 0.999858 * jax.random.normal(jax.random.fold_in(_gk, 11), (212500, 64), jnp.float32)
        return (x, src, dst, edge_attr_64)
    x, src, dst, edge_attr_64 = _rec_inputs()

    def _L0_gnn_setup():
        import jax, jax.numpy as jnp
        import numpy as np
        N = 12500
        NE = 200000
        IN_DIM = 64
        OUT_DIM = 64
        H = 8
        D = OUT_DIM // H
        key = jax.random.key(seed)
        ks = jax.random.split(key, 12)
        s = 1.0 / np.sqrt(IN_DIM)
        x = jax.random.normal(ks[0], (N, IN_DIM), jnp.float32)
        edge_attr = jax.random.normal(ks[1], (NE, IN_DIM), jnp.float32)
        edge_index = jax.random.randint(ks[2], (2, NE), 0, N, dtype=jnp.int32)
        WQ = jax.random.normal(ks[3], (IN_DIM, OUT_DIM), jnp.float32) * s
        WK = jax.random.normal(ks[4], (IN_DIM, OUT_DIM), jnp.float32) * s
        WE = jax.random.normal(ks[5], (IN_DIM, OUT_DIM), jnp.float32) * s
        WV = jax.random.normal(ks[6], (IN_DIM, OUT_DIM), jnp.float32) * s
        bQ = jax.random.normal(ks[7], (OUT_DIM,), jnp.float32) * 0.01
        bK = jax.random.normal(ks[8], (OUT_DIM,), jnp.float32) * 0.01
        bE = jax.random.normal(ks[9], (OUT_DIM,), jnp.float32) * 0.01
        bV = jax.random.normal(ks[10], (OUT_DIM,), jnp.float32) * 0.01
        return {'x': x, 'edge_attr': edge_attr, 'edge_index': edge_index, 'WQ': WQ, 'bQ': bQ, 'WK': WK, 'bK': bK, 'WE': WE, 'bE': bE, 'WV': WV, 'bV': bV}
    _L0_gnn_all = _L0_gnn_setup()
    _L0_gnn_in = {k: v for k, v in _L0_gnn_all.items() if k in ('WQ', 'bQ', 'WK', 'bK', 'WE', 'bE', 'WV', 'bV')}
    del _L0_gnn_all
    return {'x': x, 'src': src, 'dst': dst, 'edge_attr_64': edge_attr_64, 'L0_gnn_WQ': _L0_gnn_in['WQ'], 'L0_gnn_bQ': _L0_gnn_in['bQ'], 'L0_gnn_WK': _L0_gnn_in['WK'], 'L0_gnn_bK': _L0_gnn_in['bK'], 'L0_gnn_WE': _L0_gnn_in['WE'], 'L0_gnn_bE': _L0_gnn_in['bE'], 'L0_gnn_WV': _L0_gnn_in['WV'], 'L0_gnn_bV': _L0_gnn_in['bV']}

def reference(x, src, dst, edge_attr_64, L0_gnn_WQ, L0_gnn_bQ, L0_gnn_WK, L0_gnn_bK, L0_gnn_WE, L0_gnn_bE, L0_gnn_WV, L0_gnn_bV):
    import jax
    import jax.numpy as jnp

    def _L0_gnn_ref(x, edge_attr, edge_index, WQ, bQ, WK, bK, WE, bE, WV, bV):
        import jax, jax.numpy as jnp
        import numpy as np
        N = 12500
        NE = 200000
        IN_DIM = 64
        OUT_DIM = 64
        H = 8
        D = OUT_DIM // H
        n = x.shape[0]
        Qh = (x @ WQ + bQ).reshape(n, H, D)
        Kh = (x @ WK + bK).reshape(n, H, D)
        Vh = (x @ WV + bV).reshape(n, H, D)
        Eh = (edge_attr @ WE + bE).reshape(-1, H, D)
        src = edge_index[0]
        dst = edge_index[1]
        inv_sqrt_d = jnp.float32(1.0 / np.sqrt(D))
        score = Kh[src] * Qh[dst] * inv_sqrt_d * Eh
        score = jnp.exp(jnp.clip(score.sum(-1, keepdims=True), -5.0, 5.0))
        msg = Vh[src] * score
        wV = jax.ops.segment_sum(msg, dst, num_segments=n)
        return wV.reshape(n, H * D)
    edge_index = jnp.stack([src, dst])
    h = jnp.maximum(_layernorm(x, axis=-1), 0.0)
    x = x + _L0_gnn_ref(h, edge_attr_64, edge_index, L0_gnn_WQ, L0_gnn_bQ, L0_gnn_WK, L0_gnn_bK, L0_gnn_WE, L0_gnn_bE, L0_gnn_WV, L0_gnn_bV)
    return x

_drawn_inputs = setup_inputs


def setup_inputs(seed=0):
    import zlib

    import numpy as np

    out = dict(_drawn_inputs(seed))
    spreads = {}
    factors = {'L0_gnn_bQ': 8.0, 'L0_gnn_bK': 8.0, 'L0_gnn_bE': 8.0}
    for name, (base, spread) in spreads.items():
        noise = np.random.default_rng([zlib.crc32(name.encode()), seed]).standard_normal(out[name].shape)
        drawn = base * np.exp(spread * noise) if base else spread * noise
        out[name] = jnp.asarray(drawn.astype(out[name].dtype))
    for name, factor in factors.items():
        out[name] = (out[name] * factor).astype(out[name].dtype)
    return out
```

```python
from contextlib import ExitStack

import numpy as np
import concourse.bass as bass
from concourse import mybir

FP32, BF16 = mybir.dt.float32, mybir.dt.bfloat16
I32, U32 = mybir.dt.int32, mybir.dt.uint32
ALU = mybir.AluOpType
ACT = mybir.ActivationFunctionType
AX = mybir.AxisListType

N, F, E = 12500, 64, 212500
H = 8
D = F // H
P = 128
EPS = 1e-5
CLIP = 5.0
INV_SQRT_D = float(np.float32(1.0 / np.sqrt(D)))

NP, NPP = 125, 100
CT = 10
NCHUNK = NPP // CT
PAIRS = CT // 2
CF = CT * F
CUTS = [(0, 112), (112, NP)]

G = 4
GROUP = P * G
HALVES = 2
TILES = HALVES * G
SUPER = HALVES * GROUP
NSUPER = -(-E // SUPER)
TAIL = E - SUPER
OVERLAP = (NSUPER - 1) * SUPER - TAIL
NGROUP = NSUPER * HALVES
FULL = NGROUP - HALVES
GP = 104
GQ = NGROUP // GP
WINDOW = 64
NWINDOW = -(-N // WINDOW)
UNROLL = 4
NITER = NSUPER // UNROLL
IDX_AHEAD = 2
assert GP * GQ == NGROUP and NITER * UNROLL == NSUPER and OVERLAP % G == 0
assert NP * NPP == N and NCHUNK * CT == NPP and NCHUNK % 2 == 0


def build(nc, x, src, dst, edge_attr, WQ, bQ, WK, bK, WE, bE, WV, bV, out):
    kv_table = nc.dram_tensor("kv_table", (N, 2 * F), FP32).ap()
    q_table = nc.dram_tensor("q_table", (N + WINDOW, F), FP32).ap()

    ctx = ExitStack()
    with ctx:
        def sb(name, shape, dt=FP32):
            return ctx.enter_context(nc.sbuf_tensor(name, shape, dt))

        def sem(name):
            return ctx.enter_context(nc.semaphore(name))

        def sems(name, n):
            return [sem(f"{name}{k}") for k in range(n)]

        ident = sb("ident", [P, P])
        ident2 = sb("ident2", [P, F])
        iota_i = sb("iota_i", [P, WINDOW], I32)
        iota_w = sb("iota_w", [P, WINDOW])
        ones3 = sb("ones3", [3, P], BF16)
        ones_col = sb("ones_col", [P, 1])
        zeros = sb("zeros", [WINDOW, F])
        eps_col = sb("eps_col", [P, 1])
        w_node = sb("w_node", [P, 2, 3 * F])
        w_edge = sb("w_edge", [P, 2, F])
        NB = 3 * F + F
        b_row = sb("b_row", [1, NB])
        b_rest = sb("b_rest", [1, NB])
        b_part = [sb(f"b_part{k}", [1, NB], BF16) for k in range(3)]
        b3 = sb("b3", [3, NB], BF16)
        b3_node = sb("b3_node", [3, 2, 3 * F], BF16)
        b3_edge = sb("b3_edge", [3, TILES, F], BF16)
        x_sb = sb("x_sb", [NP, NPP * F])
        row_sum = sb("row_sum", [NP, 2, CT])
        centred = sb("centred", [NP, 2, CF])
        squared = sb("squared", [NP, 2, CF])
        sq_sum = sb("sq_sum", [NP, 2, CT])
        std = sb("std", [NP, 2, CT])
        rstd = sb("rstd", [NP, 2, CT])
        h_sb = sb("h_sb", [NP, 2, CF])
        hT_sb = sb("hT_sb", [P, 2, PAIRS, NP])
        rows_sb = sb("rows_sb", [NP, 2, CT, 3 * F])
        acc = sb("acc", [P, N + WINDOW])
        index_rows = [acc[0:GP, k * GQ * GROUP:(k + 1) * GQ * GROUP] for k in range(5)]
        src_rows, dst_rows = (a.bitcast(I32).rearrange("r (q e) -> r q e", q=GQ) for a in index_rows[0:2])
        src_f, dst_f, rel_rows = (a.rearrange("r (q e) -> r q e", q=GQ) for a in index_rows[2:5])
        base_i = sb("base_i", [1, NGROUP], I32)
        src_idx = sb("src_idx", [P, NGROUP + HALVES * IDX_AHEAD, G], U32)
        dst_rel = sb("dst_rel", [P, NGROUP, G])
        idx_slot = [sb(f"idx_slot{k}", [P, TILES], U32) for k in range(UNROLL)]
        kv = [sb(f"kv{k}", [P, TILES, 2 * F]) for k in range(UNROLL)]
        attr = [sb(f"attr{k}", [P, HALVES, G, F]) for k in range(2)]
        attrT = [sb(f"attrT{k}", [P, G, P]) for k in range(2)]
        onehot = [sb(f"onehot{k}", [P, G, HALVES, WINDOW]) for k in range(UNROLL)]
        onehotT = [sb(f"onehotT{k}", [P, G, P]) for k in range(2)]
        q_win = [sb(f"q_win{k}", [P, HALVES, F]) for k in range(2)]
        prod = sb("prod", [P, TILES, F])
        logits = sb("logits", [P, TILES, H])
        clipped = sb("clipped", [P, TILES, H])
        weight = sb("weight", [P, TILES, H])
        msg = [sb(f"msg{k}", [P, G, HALVES, F]) for k in range(2)]

        bank = [ctx.enter_context(nc.psum_tensor(f"bank{k}", [P, 512], FP32)) for k in range(3)]
        wide = ctx.enter_context(nc.psum_tensor("wide", [P, 1024], FP32))
        bank += [ctx.enter_context(nc.psum_tensor(f"bank{k}", [P, 512], FP32)) for k in range(3, 6)]
        hT_ps = wide[:, 0:PAIRS * P].rearrange("p (a n) -> p a n", n=P)
        node_ps = bank[0:5]
        idx_ps = bank[5]
        attrT_ps = wide[:, 0:512].rearrange("p (a n) -> p a n", n=P)
        onehotT_ps = wide[:, 512:1024].rearrange("p (a n) -> p a n", n=P)
        e_ps = bank[0:2]
        qe_ps = bank[2:4]
        sum_ps = bank[4]

        zeroed, weights_loaded, bias_loaded = sem("zeroed"), sem("weights_loaded"), sem("bias_loaded")
        pool_const, dve_const = sem("pool_const"), sem("dve_const")
        split_step, bias_split, bias_rows, bias_spread = (sem(n) for n in ("split_step", "bias_split", "bias_rows", "bias_spread"))
        pad_stored = sem("pad_stored")
        x_loaded = sems("x_loaded", 2)
        summed, centred_done, squared_done, sq_summed = (sem(n) for n in ("summed", "centred_done", "squared_done", "sq_summed"))
        std_done, rstd_done, h_done = sem("std_done"), sem("rstd_done"), sem("h_done")
        hT_done, hT_copied, rows_done, rows_copied = (sem(n) for n in ("hT_done", "hT_copied", "rows_done", "rows_copied"))
        table_stored = sems("table_stored", 2)
        src_loaded, dst_loaded, base_loaded = sem("src_loaded"), sem("dst_loaded"), sem("base_loaded")
        idx_cast, dst_cast, rel_cast = sem("idx_cast"), sem("dst_cast"), sem("rel_cast")
        idx_turned, idx_kept, masked = sem("idx_turned"), sem("idx_kept"), sem("masked")
        attr_loaded, q_loaded = sems("attr_loaded", 2), sems("q_loaded", 2)
        gather_begun, kv_gathered = sem("gather_begun"), sems("kv_gathered", UNROLL)
        idx_staged, onehot_built, ke_done, keq_done = (sem(n) for n in ("idx_staged", "onehot_built", "ke_done", "keq_done"))
        logits_done, clip_done, weight_done, msg_done, added = (sem(n) for n in ("logits_done", "clip_done", "weight_done", "msg_done", "added"))
        attrT_done, attrT_copied, onehotT_done, onehotT_copied = (sem(n) for n in ("attrT_done", "attrT_copied", "onehotT_done", "onehotT_copied"))
        e_done, qe_done, sums_done = sem("e_done"), sem("qe_done"), sem("sums_done")
        acc_zeroed = sem("acc_zeroed")
        out_turned, out_added, out_stored = sem("out_turned"), sem("out_added"), sem("out_stored")

        x_v = x.rearrange("(p t) f -> p (t f)", p=NP)
        out_v = out.rearrange("(p t) f -> p (t f)", p=NP)
        kv_v = kv_table.rearrange("(p t) f -> p t f", p=NP)
        q_v = q_table[0:N, :].rearrange("(p t) f -> p t f", p=NP)

        block = ctx.enter_context(nc.Block())

        @block.sync
        def _(sp):
            def load_x(c, i, s):
                if not isinstance(i, int) or i > 0:
                    sp.wait_ge(x_loaded[s], 32 * i)
                for a, b in CUTS:
                    sp.dma_start(x_sb[a:b, bass.ds(c * CF, CF)], x_v[a:b, bass.ds(c * CF, CF)]).then_inc(x_loaded[s], 16)

            load_x(0, 0, 0)
            load_x(1, 0, 1)
            sp.wait_ge(zeroed, 1)
            for blk in range(2):
                rows = slice(blk * F, (blk + 1) * F)
                for k, w in enumerate((WK, WV, WQ)):
                    sp.dma_start(w_node[rows, blk, k * F:(k + 1) * F], w).then_inc(weights_loaded, 16)
                sp.dma_start(w_edge[rows, blk, :], WE).then_inc(weights_loaded, 16)
            with sp.Fori(1, NCHUNK // 2) as i:
                load_x(2 * i, i, 0)
                load_x(2 * i + 1, i, 1)

            with sp.Fori(0, NCHUNK // 2) as i:
                for s in range(2):
                    c = 2 * i + s
                    sp.wait_ge(rows_copied, PAIRS * (c + 1))
                    for a, b in CUTS:
                        sp.dma_start(kv_v[a:b, bass.ds(c * CT, CT), :], rows_sb[a:b, s, :, 0:2 * F]).then_inc(table_stored[s], 16)
                        sp.dma_start(q_v[a:b, bass.ds(c * CT, CT), :], rows_sb[a:b, s, :, 2 * F:]).then_inc(table_stored[s], 16)

            def load_attr(first_edge, s):
                sp.dma_start(attr[s].rearrange("p h g f -> p h (g f)"),
                             edge_attr[bass.ds(first_edge, SUPER), :].rearrange("(h p g) f -> p h (g f)", h=HALVES, g=G)
                             ).then_inc(attr_loaded[s], 16)

            def load_q(base, s):
                for half in range(HALVES):
                    rows = slice(half * F, half * F + WINDOW)
                    sp.dma_start(q_win[s][rows, half, :], q_table[bass.ds(base[half], WINDOW), :]).then_inc(q_loaded[s], 16)

            def loads(sup, first_edge, k, slots_used):
                base = [sp.value_load(base_i[0:1, bass.ds(HALVES * sup + h, 1)], min_val=0, max_val=N - 1) for h in range(HALVES)]
                if slots_used:
                    sp.wait_ge(attrT_done, sup - 1)
                load_attr(first_edge, k % 2)
                if slots_used:
                    sp.wait_ge(qe_done, sup - 1)
                load_q(base, k % 2)

            sp.wait_ge(base_loaded, 32)
            sp.wait_ge(pad_stored, 16)
            for s in range(2):
                sp.wait_ge(table_stored[s], 64 * (NCHUNK // 2))
            for k in range(UNROLL):
                loads(k, k * SUPER, k, k >= 2)
            with sp.Fori(1, NITER - 1) as i:
                for k in range(UNROLL):
                    loads(UNROLL * i + k, (UNROLL * i + k) * SUPER, k, True)
            for k in range(UNROLL):
                sup = NSUPER - UNROLL + k
                loads(sup, sup * SUPER if sup < NSUPER - 1 else TAIL, k, True)

            for c in range(NCHUNK):
                sp.wait_ge(out_added, c + 1)
                for a, b in CUTS:
                    sp.dma_start(out_v[a:b, c * CF:(c + 1) * CF], x_sb[a:b, c * CF:(c + 1) * CF]).then_inc(out_stored, 16)
            sp.wait_ge(out_stored, 32 * NCHUNK)

        @block.gpsimd
        def _(pool):
            nc.gpsimd.memset(w_node[:], 0.0)
            nc.gpsimd.memset(w_edge[:], 0.0).then_inc(zeroed, 1)
            nc.gpsimd.iota(iota_i[:, :], pattern=[[1, WINDOW]], base=0, channel_multiplier=0)
            nc.gpsimd.memset(ident[:], 0.0)
            nc.gpsimd.memset(ident2[:], 0.0)
            nc.gpsimd.memset(zeros[:], 0.0)
            nc.gpsimd.memset(q_win[0][:], 0.0)
            nc.gpsimd.memset(q_win[1][:], 0.0)
            nc.gpsimd.memset(src_idx[:, NGROUP:, :], 0).then_inc(pool_const, 1)
            pool.wait_ge(pool_const, 1)
            nc.gpsimd.affine_select(out=ident[:], in_=ident[:], compare_op=ALU.not_equal, fill=1.0, base=0,
                                    pattern=[[-1, P]], channel_multiplier=1)
            nc.gpsimd.affine_select(out=ident2[:], in_=ident2[:], compare_op=ALU.not_equal, fill=1.0, base=0,
                                    pattern=[[-1, F]], channel_multiplier=1)
            nc.gpsimd.tensor_copy(iota_w[:, :], iota_i[:, :]).then_inc(pool_const, 1)
            pool.wait_ge(pool_const, 2)
            pool.dma_start(q_table[N:N + WINDOW, :], zeros[:, :]).then_inc(pad_stored, 16)
            nc.gpsimd.affine_select(out=ident2[:], in_=ident2[:], compare_op=ALU.not_equal, fill=1.0, base=-F,
                                    pattern=[[-1, F]], channel_multiplier=1).then_inc(pool_const, 1)

            pool.wait_ge(src_loaded, 48)
            nc.gpsimd.tensor_copy(src_f, src_rows).then_inc(idx_cast, 1)
            pool.wait_ge(dst_loaded, 48)
            nc.gpsimd.tensor_copy(dst_f, dst_rows).then_inc(dst_cast, 1)
            pool.wait_ge(dst_cast, 1)
            nc.gpsimd.tensor_tensor(rel_rows, dst_f, dst_f[:, :, 0:1].to_broadcast([GP, GQ, GROUP]), ALU.subtract).then_inc(rel_cast, 1)

            def gather(sup, k, slot_used):
                pool.wait_ge(idx_staged, sup + 1)
                if slot_used:
                    pool.wait_ge(msg_done, sup + 1 - UNROLL)
                pool.sem_inc(gather_begun, 1)
                for t in range(TILES):
                    pool.indirect_dma_start(kv[k][:, t, :], None, kv_table,
                                            bass.IndirectOffsetOnAxis(idx_slot[k][:, t:t + 1], 0)).then_inc(kv_gathered[k], 16)

            for s in range(2):
                pool.wait_ge(table_stored[s], 64 * (NCHUNK // 2))
            for k in range(UNROLL):
                gather(k, k, False)
            with pool.Fori(1, NITER) as i:
                for k in range(UNROLL):
                    gather(UNROLL * i + k, k, True)

        @block.scalar
        def _(act):
            for rows, arr, done in ((src_rows, src, src_loaded), (dst_rows, dst, dst_loaded)):
                lead = (GQ - 1) * GP
                act.dma_start(rows[:, 0:GQ - 1, :], arr[0:lead * GROUP].rearrange("(q r e) -> r q e", r=GP, e=GROUP)).then_inc(done, 16)
                act.dma_start(rows[0:FULL - lead, GQ - 1, :], arr[lead * GROUP:FULL * GROUP].rearrange("(r e) -> r e", e=GROUP)).then_inc(done, 16)
                act.dma_start(rows[FULL - lead:GP, GQ - 1, :], arr[TAIL:E].rearrange("(r e) -> r e", e=GROUP)).then_inc(done, 16)
            for k, b in enumerate((bK, bV, bQ, bE)):
                act.dma_start(b_row[0:1, k * F:(k + 1) * F], b.rearrange("(o f) -> o f", o=1)).then_inc(bias_loaded, 16)
            with nc.allow_non_contiguous_dma("one dst of each group"):
                act.dma_start(base_i[0:1, 0:FULL], dst[0:FULL * GROUP].rearrange("(o j e) -> o j e", o=1, e=GROUP)[:, :, 0]).then_inc(base_loaded, 16)
                act.dma_start(base_i[0:1, FULL:NGROUP], dst[TAIL:E].rearrange("(o j e) -> o j e", o=1, e=GROUP)[:, :, 0]).then_inc(base_loaded, 16)
            act.wait_ge(bias_split, 1)
            for k in range(3):
                act.dma_start(b3[k:k + 1, :], b_part[k][0:1, :]).then_inc(bias_rows, 16)
            act.wait_ge(dve_const, 1)

            def node_chunks(i, first):
                for s in range(2):
                    c = 2 * i + s
                    act.wait_ge(centred_done, c + 1)
                    if not first:
                        act.wait_ge(sq_summed, c - 1)
                    nc.scalar.activation(squared[:, s, :], centred[:, s, :], ACT.Square).then_inc(squared_done, 1)
                for s in range(2):
                    c = 2 * i + s
                    act.wait_ge(sq_summed, c + 1)
                    if not first:
                        act.wait_ge(rstd_done, c - 1)
                    nc.scalar.activation(std[:, s, :], sq_sum[:, s, :], ACT.Sqrt, scale=1.0 / F, bias=eps_col[0:NP, :]).then_inc(std_done, 1)
                for s in range(2):
                    c = 2 * i + s
                    act.wait_ge(hT_done, c + 1)
                    if not first:
                        act.wait_ge(rows_done, PAIRS * (c - 1))
                    nc.scalar.copy(hT_sb[:, s, :, :], hT_ps[:, :, 0:NP]).then_inc(hT_copied, 1)
                    if not first:
                        act.wait_ge(table_stored[s], 64 * i)
                    for a in range(PAIRS):
                        act.wait_ge(rows_done, PAIRS * c + a + 1)
                        nc.scalar.copy(rows_sb[:, s, 2 * a:2 * a + 2, :].rearrange("p t f -> p (t f)"),
                                       node_ps[a][0:NP, 0:6 * F]).then_inc(rows_copied, 1)

            node_chunks(0, True)
            with act.Fori(1, NCHUNK // 2) as i:
                node_chunks(i, False)

            def turned(sup, k, slot_used):
                act.wait_ge(attrT_done, sup + 1)
                if slot_used:
                    act.wait_ge(e_done, sup - 1)
                nc.scalar.copy(attrT[k % 2][:], attrT_ps).then_inc(attrT_copied, 1)
                act.wait_ge(onehotT_done, sup + 1)
                if slot_used:
                    act.wait_ge(qe_done, sup - 1)
                nc.scalar.copy(onehotT[k % 2][:], onehotT_ps).then_inc(onehotT_copied, 1)

            def weights(sup, first):
                act.wait_ge(clip_done, sup + 1)
                if not first:
                    act.wait_ge(msg_done, sup)
                nc.scalar.activation(weight[:], clipped[:], ACT.Exp).then_inc(weight_done, 1)

            for k in range(UNROLL):
                turned(k, k, k >= 2)
                if k > 0:
                    weights(k - 1, k == 1)
            with act.Fori(1, NITER) as i:
                for k in range(UNROLL):
                    turned(UNROLL * i + k, k, True)
                    weights(UNROLL * i + k - 1, False)
            weights(NSUPER - 1, False)

        @block.vector
        def _(dve):
            nc.vector.memset(eps_col[:], EPS).then_inc(dve_const, 1)
            nc.vector.memset(ones3[:], 1.0).then_inc(dve_const, 1)
            nc.vector.memset(ones_col[:], 1.0).then_inc(dve_const, 1)
            dve.wait_ge(bias_loaded, 64)
            nc.vector.tensor_copy(b_part[0][:], b_row[:]).then_inc(split_step, 1)
            dve.wait_ge(split_step, 1)
            nc.vector.tensor_tensor(b_rest[:], b_row[:], b_part[0][:], ALU.subtract).then_inc(split_step, 1)
            dve.wait_ge(split_step, 2)
            nc.vector.tensor_copy(b_part[1][:], b_rest[:]).then_inc(split_step, 1)
            dve.wait_ge(split_step, 3)
            nc.vector.tensor_tensor(b_part[2][:], b_rest[:], b_part[1][:], ALU.subtract).then_inc(bias_split, 1)
            dve.wait_ge(bias_rows, 48)
            for t in range(2):
                nc.vector.tensor_copy(b3_node[:, t, :], b3[:, 0:3 * F])
            nc.vector.tensor_copy(b3_edge[:], b3[:, None, 3 * F:].to_broadcast([3, TILES, F])).then_inc(bias_spread, 1)

            def node_chunks(i, first):
                for s in range(2):
                    c = 2 * i + s
                    xc = x_sb[:, bass.ds(c * CF, CF)].rearrange("p (t f) -> p t f", f=F)
                    dve.wait_ge(x_loaded[s], 32 * (i + 1))
                    nc.vector.tensor_reduce(row_sum[:, s, :], xc, AX.X, ALU.add).then_inc(summed, 1)
                    dve.wait_ge(summed, c + 1)
                    nc.vector.scalar_tensor_tensor(
                        out=centred[:, s, :].rearrange("p (t f) -> p t f", f=F),
                        in0=row_sum[:, s, :, None].to_broadcast([NP, CT, F]), scalar=-1.0 / F, in1=xc,
                        op0=ALU.mult, op1=ALU.add).then_inc(centred_done, 1)
                for s in range(2):
                    c = 2 * i + s
                    dve.wait_ge(squared_done, c + 1)
                    nc.vector.tensor_reduce(sq_sum[:, s, :], squared[:, s, :].rearrange("p (t f) -> p t f", f=F),
                                            AX.X, ALU.add).then_inc(sq_summed, 1)
                for s in range(2):
                    c = 2 * i + s
                    dve.wait_ge(std_done, c + 1)
                    nc.vector.reciprocal(rstd[:, s, :], std[:, s, :]).then_inc(rstd_done, 1)
                    dve.wait_ge(rstd_done, c + 1)
                    if not first:
                        dve.wait_ge(hT_done, c - 1)
                    nc.vector.scalar_tensor_tensor(
                        out=h_sb[:, s, :].rearrange("p (t f) -> p t f", f=F),
                        in0=centred[:, s, :].rearrange("p (t f) -> p t f", f=F), scalar=0.0,
                        in1=rstd[:, s, :, None].to_broadcast([NP, CT, F]),
                        op0=ALU.max, op1=ALU.mult).then_inc(h_done, 1)

            node_chunks(0, True)
            with dve.Fori(1, NCHUNK // 2) as i:
                node_chunks(i, False)

            for q in range(GQ):
                dve.wait_ge(idx_turned, q + 1)
                nc.vector.tensor_copy(src_idx[:, q * GP:(q + 1) * GP, :].rearrange("p r g -> p g r"),
                                      idx_ps[:, 0:G * GP].rearrange("p (g r) -> p g r", g=G)).then_inc(idx_kept, 1)
            for q in range(GQ):
                dve.wait_ge(idx_turned, GQ + q + 1)
                nc.vector.tensor_copy(dst_rel[:, q * GP:(q + 1) * GP, :].rearrange("p r g -> p g r"),
                                      idx_ps[:, 0:G * GP].rearrange("p (g r) -> p g r", g=G)).then_inc(idx_kept, 1)
            dve.wait_ge(idx_kept, 2 * GQ)
            nc.vector.memset(dst_rel[0:OVERLAP // G, FULL, :], -1.0).then_inc(masked, 1)
            nc.vector.memset(acc[:], 0.0).then_inc(acc_zeroed, 1)
            dve.wait_ge(masked, 1)
            dve.wait_ge(acc_zeroed, 1)
            dve.wait_ge(pool_const, 2)

            def stage_idx(sup, k):
                nc.vector.tensor_copy(idx_slot[k % UNROLL][:].rearrange("p (g h) -> p h g", g=G),
                                      src_idx[:, bass.ds(HALVES * sup, HALVES), :]).then_inc(idx_staged, 1)

            def build_onehot(sup, k, slot_used):
                if slot_used:
                    dve.wait_ge(sums_done, sup - UNROLL + 1)
                nc.vector.tensor_tensor(
                    onehot[k][:],
                    iota_w[:, None, None, :].to_broadcast([P, G, HALVES, WINDOW]),
                    dst_rel[:, bass.ds(HALVES * sup, HALVES), :].rearrange("p h g -> p g h")[:, :, :, None].to_broadcast([P, G, HALVES, WINDOW]),
                    ALU.is_equal).then_inc(onehot_built, 1)

            def messages(sup, rounds, k):
                s = k % 2
                dve.wait_ge(kv_gathered[k], 16 * TILES * rounds)
                stage_idx(sup + IDX_AHEAD, k + IDX_AHEAD)
                dve.wait_ge(e_done, sup + 1)
                nc.vector.tensor_tensor(prod[:], kv[k][:, :, 0:F], e_ps[s].rearrange("p (t f) -> p t f", f=F),
                                        ALU.mult).then_inc(ke_done, 1)
                dve.wait_ge(ke_done, sup + 1)
                dve.wait_ge(qe_done, sup + 1)
                nc.vector.scalar_tensor_tensor(
                    out=prod[:].rearrange("p t f -> p (t f)"), in0=prod[:].rearrange("p t f -> p (t f)"),
                    scalar=INV_SQRT_D, in1=qe_ps[s][:], op0=ALU.mult, op1=ALU.mult).then_inc(keq_done, 1)
                dve.wait_ge(keq_done, sup + 1)
                nc.vector.tensor_reduce(logits[:], prod[:].rearrange("p t (h d) -> p t h d", d=D), AX.X, ALU.add).then_inc(logits_done, 1)
                dve.wait_ge(logits_done, sup + 1)
                nc.vector.tensor_scalar(clipped[:], logits[:], CLIP, -CLIP, ALU.min, ALU.max).then_inc(clip_done, 1)
                dve.wait_ge(weight_done, sup + 1)
                nc.vector.tensor_tensor(
                    msg[s].rearrange("p g h (a d) -> p (g h) a d", d=D),
                    kv[k][:, :, F:].rearrange("p t (a d) -> p t a d", d=D),
                    weight[:, :, :, None].to_broadcast([P, TILES, H, D]), ALU.mult).then_inc(msg_done, 1)

            def add_sums(sup, first):
                base = [dve.value_load(base_i[0:1, bass.ds(HALVES * sup + h, 1)], min_val=0, max_val=N - 1) for h in range(HALVES)]
                dve.wait_ge(sums_done, sup + 1)
                if not first:
                    dve.wait_ge(added, HALVES * sup)
                for half in range(HALVES):
                    rows = slice(half * F, (half + 1) * F)
                    win = acc[rows, bass.ds(base[half], WINDOW)]
                    nc.vector.tensor_tensor(win, win, sum_ps[rows, half * WINDOW:(half + 1) * WINDOW], ALU.add).then_inc(added, 1)

            for k in range(IDX_AHEAD):
                stage_idx(k, k)
            dve.wait_ge(base_loaded, 32)
            for k in range(UNROLL):
                build_onehot(k, k, False)
                if k > 0:
                    messages(k - 1, 1, k - 1)
                if k > 1:
                    add_sums(k - 2, k == 2)
            with dve.Fori(1, NITER) as i:
                for k in range(UNROLL):
                    sup = UNROLL * i + k
                    build_onehot(sup, k, True)
                    messages(sup - 1, i + 1 if k else i, (k - 1) % UNROLL)
                    add_sums(sup - 2, False)
            messages(NSUPER - 1, NITER, UNROLL - 1)
            add_sums(NSUPER - 2, False)
            add_sums(NSUPER - 1, False)

            out_ps = [wide[0:NP, 0:CF]]
            for c in range(NCHUNK):
                dve.wait_ge(out_turned, c + 1)
                nc.vector.tensor_tensor(x_sb[:, c * CF:(c + 1) * CF], x_sb[:, c * CF:(c + 1) * CF], out_ps[0], ALU.add).then_inc(out_added, 1)

        @block.tensor
        def _(pe):
            pe.wait_ge(pool_const, 3)
            pe.wait_ge(dve_const, 3)
            pe.wait_ge(bias_spread, 1)
            pe.wait_ge(weights_loaded, 16 * 8)

            def node_chunks(i, first):
                for s in range(2):
                    c = 2 * i + s
                    pe.wait_ge(h_done, c + 1)
                    if not first or s > 0:
                        pe.wait_ge(hT_copied, c)
                    for a in range(PAIRS):
                        last = nc.tensor.transpose(hT_ps[:, a, 0:NP], h_sb[:, s, 2 * a * F:2 * (a + 1) * F], ident[0:NP, 0:NP])
                    last.then_inc(hT_done, 1)
                    pe.wait_ge(hT_copied, c + 1)
                    for a in range(PAIRS):
                        if not first or s > 0:
                            pe.wait_ge(rows_copied, PAIRS * (c - 1) + a + 1)
                        rows = node_ps[a][0:NP, 0:6 * F]
                        nc.tensor.matmul(rows, ones3[:, 0:NP], b3_node[:].rearrange("k t f -> k (t f)"), start=True, stop=False)
                        nc.tensor.matmul(rows, hT_sb[:, s, a, :], w_node[:].rearrange("k t f -> k (t f)"), start=False, stop=True).then_inc(rows_done, 1)

            node_chunks(0, True)
            with pe.Fori(1, NCHUNK // 2) as i:
                node_chunks(i, False)

            for n, (rows, cast) in enumerate(((src_f, idx_cast), (rel_rows, rel_cast))):
                pe.wait_ge(cast, 1)
                for q in range(GQ):
                    if n or q:
                        pe.wait_ge(idx_kept, n * GQ + q)
                    for g in range(G):
                        last = nc.tensor.transpose(idx_ps[:, g * GP:(g + 1) * GP],
                                                   rows[:, q, :].rearrange("r (p g) -> r g p", g=G)[:, g, :], ident[0:GP, 0:GP])
                    last.then_inc(idx_turned, 1)
            pe.wait_ge(idx_kept, 2 * GQ)
            pe.wait_ge(rows_copied, PAIRS * NCHUNK)

            def expand(i, k, first):
                sup = UNROLL * i + k
                s = k % 2
                pe.wait_ge(attr_loaded[s], 16 * (UNROLL // 2 * i + k // 2 + 1))
                if not first or k > 0:
                    pe.wait_ge(attrT_copied, sup)
                for g in range(G):
                    last = nc.tensor.transpose(attrT_ps[:, g, :], attr[s].rearrange("p h g f -> p (h g f)")[:, 2 * g * F:2 * (g + 1) * F], ident[:])
                last.then_inc(attrT_done, 1)
                pe.wait_ge(onehot_built, sup + 1)
                if not first or k > 0:
                    pe.wait_ge(onehotT_copied, sup)
                for g in range(G):
                    last = nc.tensor.transpose(onehotT_ps[:, g, :], onehot[k][:, g, :, :].rearrange("p h w -> p (h w)"), ident[:])
                last.then_inc(onehotT_done, 1)
                pe.wait_ge(attrT_copied, sup + 1)
                if not first or k >= 2:
                    pe.wait_ge(ke_done, sup - 1)
                nc.tensor.matmul(e_ps[s][:], ones3[:, :], b3_edge[:].rearrange("k t f -> k (t f)"), start=True, stop=False)
                for a in range(G):
                    half, pair = a // 2, a % 2
                    last = nc.tensor.matmul(
                        e_ps[s].rearrange("p (g h f) -> p h g f", g=G, h=HALVES)[:, half, 2 * pair:2 * pair + 2, :],
                        attrT[s][:, a, :], w_edge[:], start=False, stop=a == G - 1)
                last.then_inc(e_done, 1)
                pe.wait_ge(onehotT_copied, sup + 1)
                pe.wait_ge(q_loaded[s], 32 * (UNROLL // 2 * i + k // 2 + 1))
                if not first or k >= 2:
                    pe.wait_ge(keq_done, sup - 1)
                for g in range(G):
                    last = nc.tensor.matmul(qe_ps[s][:, 2 * g * F:2 * (g + 1) * F],
                                            onehotT[s][:, g, :], q_win[s].rearrange("k h f -> k (h f)"), start=True, stop=True)
                last.then_inc(qe_done, 1)

            def sum_messages(sup, k, first):
                pe.wait_ge(msg_done, sup + 1)
                if not first:
                    pe.wait_ge(added, HALVES * sup)
                for g in range(G):
                    last = nc.tensor.matmul(sum_ps[:, 0:HALVES * WINDOW], msg[k % 2][:, g, :, :].rearrange("p h f -> p (h f)"),
                                            onehot[k][:, g, :, :].rearrange("p h w -> p (h w)"), start=g == 0, stop=g == G - 1)
                last.then_inc(sums_done, 1)

            for k in range(UNROLL):
                expand(0, k, True)
                if k > 0:
                    sum_messages(k - 1, k - 1, k == 1)
            with pe.Fori(1, NITER) as i:
                for k in range(UNROLL):
                    expand(i, k, False)
                    sum_messages(UNROLL * i + k - 1, (k - 1) % UNROLL, False)
            sum_messages(NSUPER - 1, UNROLL - 1, False)

            pe.wait_ge(added, HALVES * NSUPER)
            pe.wait_ge(onehotT_copied, NSUPER)
            for c in range(NCHUNK):
                if c:
                    pe.wait_ge(out_added, c)
                for t in range(CT):
                    last = nc.tensor.matmul(wide[0:NP, t * F:(t + 1) * F],
                                            acc[:, 0:N].rearrange("p (n t) -> p t n", t=NPP)[:, c * CT + t, :], ident2[:], start=True, stop=True)
                last.then_inc(out_turned, 1)


_INS = ["x", "src", "dst", "edge_attr_64", "L0_gnn_WQ", "L0_gnn_bQ", "L0_gnn_WK", "L0_gnn_bK",
        "L0_gnn_WE", "L0_gnn_bE", "L0_gnn_WV", "L0_gnn_bV"]


def kernel(**inputs):
    import concourse.bacc as _bacc
    from concourse.bass_utils import run_bass_kernel_spmd as _run

    nc = _bacc.Bacc("TRN2", target_bir_lowering=False, num_devices=1)
    arrays, args = {}, []
    for name in _INS:
        a = np.ascontiguousarray(inputs[name])
        arrays[f"in_{name}"] = a
        args.append(nc.dram_tensor(f"in_{name}", a.shape, mybir.dt.from_np(a.dtype), kind="ExternalInput").ap())
    out = nc.dram_tensor("out_0", (N, F), FP32, kind="ExternalOutput").ap()
    build(nc, *args, out)
    r = _run(nc, [arrays], core_ids=[0])
    return r.results[0]["out_0"]
```

```python
from contextlib import ExitStack

import numpy as np
import concourse.bass as bass
from concourse import mybir

FP32, BF16 = mybir.dt.float32, mybir.dt.bfloat16
I32, U32 = mybir.dt.int32, mybir.dt.uint32
ALU = mybir.AluOpType
ACT = mybir.ActivationFunctionType
AX = mybir.AxisListType

N, F, E = 12500, 64, 212500
H = 8
D = F // H
P = 128
EPS = 1e-5
CLIP = 5.0
INV_SQRT_D = float(np.float32(1.0 / np.sqrt(D)))

NP, NPP = 125, 100
CT = 10
NCHUNK = NPP // CT
PAIRS = CT // 2
CF = CT * F
OUT_STEPS = [(t, min(t + 8, NPP)) for t in range(0, NPP, 8)]
X_LOADS = [(0, 2), (2, 4), (4, NCHUNK)]
CUTS = [(0, 112), (112, NP)]

G = 4
GROUP = P * G
HALVES = 2
TILES = HALVES * G
SUPER = HALVES * GROUP
NSUPER = -(-E // SUPER)
TAIL = E - SUPER
OVERLAP = (NSUPER - 1) * SUPER - TAIL
NGROUP = NSUPER * HALVES
FULL = NGROUP - HALVES
GP = 104
GQ = NGROUP // GP
WINDOW = 64
NWINDOW = -(-N // WINDOW)
UNROLL = 4
NITER = NSUPER // UNROLL
assert GP * GQ == NGROUP and NITER * UNROLL == NSUPER and OVERLAP % G == 0
assert NP * NPP == N and NCHUNK * CT == NPP and NCHUNK % 2 == 0


def build(nc, x, src, dst, edge_attr, WQ, bQ, WK, bK, WE, bE, WV, bV, out):
    kv_table = nc.dram_tensor("kv_table", (N, 2 * F), FP32).ap()
    q_table = nc.dram_tensor("q_table", (N + WINDOW, F), FP32).ap()

    ctx = ExitStack()
    with ctx:
        def sb(name, shape, dt=FP32):
            return ctx.enter_context(nc.sbuf_tensor(name, shape, dt))

        def sem(name):
            return ctx.enter_context(nc.semaphore(name))

        def sems(name, n):
            return [sem(f"{name}{k}") for k in range(n)]

        ident = sb("ident", [P, P])
        iota_i = sb("iota_i", [P, WINDOW], I32)
        iota_w = sb("iota_w", [P, WINDOW])
        ones3 = sb("ones3", [3, P], BF16)
        ones_col = sb("ones_col", [P, 1])
        zeros = sb("zeros", [WINDOW, F])
        eps_col = sb("eps_col", [P, 1])
        w_node = sb("w_node", [P, 2, 3 * F])
        w_edge = sb("w_edge", [P, 2, F])
        NB = 3 * F + F
        b_all = sb("b_all", [3, NB])
        b_rest = sb("b_rest", [3, NB])
        b_part = [sb(f"b_part{k}", [3, NB], BF16) for k in range(3)]
        b_pick = sb("b_pick", [3, NB], BF16)
        b3 = sb("b3", [3, NB], BF16)
        b3_node = sb("b3_node", [3, 2, 3 * F], BF16)
        b3_edge = sb("b3_edge", [3, TILES, F], BF16)
        x_sb = sb("x_sb", [NP, NPP * F])
        row_sum = sb("row_sum", [NP, NPP])
        centred = sb("centred", [NP, NPP * F])
        squared = [sb(f"squared{k}", [NP, CF]) for k in range(2)]
        sq_sum = sb("sq_sum", [NP, NPP])
        std = sb("std", [NP, NPP])
        rstd = sb("rstd", [NP, NPP])
        h_sb = [sb(f"h_sb{k}", [NP, CF]) for k in range(2)]
        hT_sb = sb("hT_sb", [P, 2, PAIRS, NP])
        rows_sb = sb("rows_sb", [NP, 2, CT, 3 * F])
        acc = sb("acc", [P, N + WINDOW])
        index_rows = [acc[0:GP, k * GQ * GROUP:(k + 1) * GQ * GROUP] for k in range(5)]
        src_rows, dst_rows = (a.bitcast(I32).rearrange("r (q e) -> r q e", q=GQ) for a in index_rows[0:2])
        src_f, dst_f, rel_rows = (a.rearrange("r (q e) -> r q e", q=GQ) for a in index_rows[2:5])
        base_i = sb("base_i", [1, NGROUP], I32)
        src_idx = sb("src_idx", [P, NGROUP + HALVES * UNROLL, G], U32)
        dst_rel = sb("dst_rel", [P, NGROUP, G])
        lowest, highest = sb("lowest", [P, 1]), sb("highest", [P, 1])
        outside = sb("outside", [P, 1])
        scattered = sb("scattered", [1, 1], I32)
        base_f = sb("base_f", [1, NGROUP])
        ones_row = sb("ones_row", [1, P])
        win_i = sb("win_i", [P, NWINDOW], I32)
        win_start = sb("win_start", [P, NWINDOW])
        dst_now = sb("dst_now", [P, TILES])
        q_idx = sb("q_idx", [P, TILES], U32)
        idx_slot = [sb(f"idx_slot{k}", [P, TILES], U32) for k in range(UNROLL)]
        kv = [sb(f"kv{k}", [P, TILES, 2 * F]) for k in range(UNROLL)]
        attr = [sb(f"attr{k}", [P, HALVES, G, F]) for k in range(2)]
        attrT = [sb(f"attrT{k}", [P, G, P]) for k in range(2)]
        onehot = [sb(f"onehot{k}", [P, G, HALVES, WINDOW]) for k in range(UNROLL)]
        onehotT = [sb(f"onehotT{k}", [P, G, P]) for k in range(2)]
        q_win = [sb(f"q_win{k}", [P, HALVES, F]) for k in range(2)]
        prod = sb("prod", [P, TILES, F])
        logits = sb("logits", [P, TILES, H])
        clipped = sb("clipped", [P, TILES, H])
        weight = sb("weight", [P, TILES, H])
        msg = [sb(f"msg{k}", [P, G, HALVES, F]) for k in range(2)]

        wide = [ctx.enter_context(nc.psum_tensor(f"wide{k}", [P, 1024], FP32)) for k in range(2)]
        bank = [ctx.enter_context(nc.psum_tensor(f"bank{k}", [P, 512], FP32))[:] for k in range(4)]
        hT_ps = wide[0][:, 0:PAIRS * P].rearrange("p (a n) -> p a n", n=P)
        node_ps = bank + [wide[1][:, 0:512]]
        idx_ps = [wide[1][:, 512:1024], wide[0][:, 0:512]]
        attrT_ps = wide[0][:, 0:512].rearrange("p (a n) -> p a n", n=P)
        onehotT_ps = wide[0][:, 512:1024].rearrange("p (a n) -> p a n", n=P)
        e_ps = bank[0:2]
        qe_ps = bank[2:4]
        sum_ps = wide[1][:, 0:512]
        base_ps = wide[1][:, 512:1024]

        zeroed, weights_loaded, edge_weights_loaded, bias_loaded = (
            sem(n) for n in ("zeroed", "weights_loaded", "edge_weights_loaded", "bias_loaded"))
        pool_const, dve_const = sem("pool_const"), sem("dve_const")
        split_step, bias_spread = sem("split_step"), sem("bias_spread")
        pad_stored = sem("pad_stored")
        x_loaded = sems("x_loaded", 3)
        summed, centred_done, squared_done, sq_summed = (sem(n) for n in ("summed", "centred_done", "squared_done", "sq_summed"))
        std_done, rstd_done, h_done = sem("std_done"), sem("rstd_done"), sem("h_done")
        hT_done, hT_copied, rows_done, rows_copied = (sem(n) for n in ("hT_done", "hT_copied", "rows_done", "rows_copied"))
        table_stored = sems("table_stored", 2)
        src_loaded, dst_loaded, base_loaded = sem("src_loaded"), sem("dst_loaded"), sem("base_loaded")
        idx_cast, dst_cast, rel_cast = sem("idx_cast"), sem("dst_cast"), sem("rel_cast")
        idx_turned, idx_kept, masked = sem("idx_turned"), sem("idx_kept"), sem("masked")
        attr_loaded, q_loaded = sems("attr_loaded", 2), sems("q_loaded", 2)
        gather_begun, kv_gathered = sem("gather_begun"), sems("kv_gathered", UNROLL)
        idx_staged, onehot_built, ke_done, keq_done = (sem(n) for n in ("idx_staged", "onehot_built", "ke_done", "keq_done"))
        logits_done, clip_done, weight_done, msg_done, added = (sem(n) for n in ("logits_done", "clip_done", "weight_done", "msg_done", "added"))
        attrT_done, attrT_copied, onehotT_done, onehotT_copied = (sem(n) for n in ("attrT_done", "attrT_copied", "onehotT_done", "onehotT_copied"))
        e_done, qe_done, sums_done = sem("e_done"), sem("qe_done"), sem("sums_done")
        acc_zeroed = sem("acc_zeroed")
        bounds_found, outside_found, outside_counted, form_known = (sem(n) for n in ("bounds_found", "outside_found", "outside_counted", "form_known"))
        base_cast, base_spread, dst_restored, dst_staged, q_gathered = (sem(n) for n in ("base_cast", "base_spread", "dst_restored", "dst_staged", "q_gathered"))
        edges_summed = sem("edges_summed")
        out_turned, out_added, out_stored = sem("out_turned"), sem("out_added"), sem("out_stored")

        def load_rows(eng, rows, arr, loaded):
            lead = (GQ - 1) * GP
            eng.dma_start(rows[:, 0:GQ - 1, :], arr[0:lead * GROUP].rearrange("(q r e) -> r q e", r=GP, e=GROUP)).then_inc(loaded, 16)
            eng.dma_start(rows[0:FULL - lead, GQ - 1, :], arr[lead * GROUP:FULL * GROUP].rearrange("(r e) -> r e", e=GROUP)).then_inc(loaded, 16)
            eng.dma_start(rows[FULL - lead:GP, GQ - 1, :], arr[TAIL:E].rearrange("(r e) -> r e", e=GROUP)).then_inc(loaded, 16)

        def any_outside(eng):
            eng.wait_ge(form_known, 1)
            return eng.value_load(scattered[0:1, 0:1], min_val=0, max_val=2 * P)

        q_rows = kv[1][:].rearrange("p t f -> p (t f)")[:, 0:TILES * F].rearrange("p (t f) -> p t f", f=F)
        x_v = x.rearrange("(p t) f -> p (t f)", p=NP)
        out_v = out.rearrange("(p t) f -> p (t f)", p=NP)
        kv_v = kv_table.rearrange("(p t) f -> p t f", p=NP)
        q_v = q_table[0:N, :].rearrange("(p t) f -> p t f", p=NP)

        block = ctx.enter_context(nc.Block())

        @block.sync
        def _(sp):
            for n, (c, end) in enumerate(X_LOADS):
                for a, b in CUTS:
                    sp.dma_start(x_sb[a:b, c * CF:end * CF], x_v[a:b, c * CF:end * CF]).then_inc(x_loaded[n], 16)
                if n == 0:
                    sp.wait_ge(zeroed, 1)
                    for blk in range(2):
                        for k, w in enumerate((WK, WV, WQ)):
                            sp.dma_start(w_node[blk * F:(blk + 1) * F, blk, k * F:(k + 1) * F], w).then_inc(weights_loaded, 16)
            load_rows(sp, src_rows, src, src_loaded)
            for blk in range(2):
                sp.dma_start(w_edge[blk * F:(blk + 1) * F, blk, :], WE).then_inc(edge_weights_loaded, 16)

            with sp.Fori(0, NCHUNK // 2) as i:
                for s in range(2):
                    c = 2 * i + s
                    sp.wait_ge(rows_copied, PAIRS * (c + 1))
                    for a, b in CUTS:
                        sp.dma_start(kv_v[a:b, bass.ds(c * CT, CT), :], rows_sb[a:b, s, :, 0:2 * F]).then_inc(table_stored[s], 16)
                        sp.dma_start(q_v[a:b, bass.ds(c * CT, CT), :], rows_sb[a:b, s, :, 2 * F:]).then_inc(table_stored[s], 16)

            def load_attr(first_edge, s):
                sp.dma_start(attr[s].rearrange("p h g f -> p h (g f)"),
                             edge_attr[bass.ds(first_edge, SUPER), :].rearrange("(h p g) f -> p h (g f)", h=HALVES, g=G)
                             ).then_inc(attr_loaded[s], 16)

            def load_q(base, s):
                for half in range(HALVES):
                    rows = slice(half * F, half * F + WINDOW)
                    sp.dma_start(q_win[s][rows, half, :], q_table[bass.ds(base[half], WINDOW), :]).then_inc(q_loaded[s], 16)

            def loads(sup, first_edge, k, slots_used):
                base = [sp.value_load(base_i[0:1, bass.ds(HALVES * sup + h, 1)], min_val=0, max_val=N - 1) for h in range(HALVES)]
                if slots_used:
                    sp.wait_ge(attrT_done, sup - 1)
                load_attr(first_edge, k % 2)
                if slots_used:
                    sp.wait_ge(qe_done, sup - 1)
                load_q(base, k % 2)

            sp.wait_ge(base_loaded, 32)
            sp.wait_ge(pad_stored, 16)
            for s in range(2):
                sp.wait_ge(table_stored[s], 64 * (NCHUNK // 2))
            with sp.If(any_outside(sp) < 1):
                for k in range(UNROLL):
                    loads(k, k * SUPER, k, k >= 2)
                with sp.Fori(1, NITER - 1) as i:
                    for k in range(UNROLL):
                        loads(UNROLL * i + k, (UNROLL * i + k) * SUPER, k, True)
                for k in range(UNROLL):
                    sup = NSUPER - UNROLL + k
                    loads(sup, sup * SUPER if sup < NSUPER - 1 else TAIL, k, True)
            with sp.Else():
                load_attr(0, 0)
                with sp.Fori(1, NSUPER - 1) as sup:
                    sp.wait_ge(attrT_done, sup)
                    load_attr(sup * SUPER, 0)
                sp.wait_ge(attrT_done, NSUPER - 1)
                load_attr(TAIL, 0)

            for c, (t, end) in enumerate(OUT_STEPS):
                sp.wait_ge(out_added, HALVES * (c + 1))
                for a, b in CUTS:
                    sp.dma_start(out_v[a:b, t * F:end * F], x_sb[a:b, t * F:end * F]).then_inc(out_stored, 16)
            sp.wait_ge(out_stored, 32 * len(OUT_STEPS))

        @block.gpsimd
        def _(pool):
            nc.gpsimd.memset(w_node[:], 0.0)
            nc.gpsimd.memset(w_edge[:], 0.0).then_inc(zeroed, 1)
            nc.gpsimd.iota(win_i[:, :], pattern=[[WINDOW, NWINDOW]], base=0, channel_multiplier=0)
            nc.gpsimd.iota(iota_i[:, :], pattern=[[1, WINDOW]], base=0, channel_multiplier=0)
            nc.gpsimd.memset(ident[:], 0.0)
            nc.gpsimd.memset(zeros[:], 0.0)
            nc.gpsimd.memset(q_win[0][:], 0.0)
            nc.gpsimd.memset(q_win[1][:], 0.0)
            nc.gpsimd.memset(src_idx[:, NGROUP:, :], 0).then_inc(pool_const, 1)
            pool.wait_ge(pool_const, 1)
            nc.gpsimd.affine_select(out=ident[:], in_=ident[:], compare_op=ALU.not_equal, fill=1.0, base=0,
                                    pattern=[[-1, P]], channel_multiplier=1)
            nc.gpsimd.tensor_copy(win_start[:, :], win_i[:, :])
            nc.gpsimd.tensor_copy(iota_w[:, :], iota_i[:, :]).then_inc(pool_const, 1)
            pool.wait_ge(pool_const, 2)
            pool.dma_start(q_table[N:N + WINDOW, :], zeros[:, :]).then_inc(pad_stored, 16)

            load_rows(pool, dst_rows, dst, dst_loaded)
            with nc.allow_non_contiguous_dma("one dst of each group"):
                pool.dma_start(base_i[0:1, 0:FULL], dst[0:FULL * GROUP].rearrange("(o j e) -> o j e", o=1, e=GROUP)[:, :, 0]).then_inc(base_loaded, 16)
                pool.dma_start(base_i[0:1, FULL:NGROUP], dst[TAIL:E].rearrange("(o j e) -> o j e", o=1, e=GROUP)[:, :, 0]).then_inc(base_loaded, 16)
            pool.wait_ge(src_loaded, 48)
            nc.gpsimd.tensor_copy(src_f, src_rows).then_inc(idx_cast, 1)
            pool.wait_ge(dst_loaded, 48)
            nc.gpsimd.tensor_copy(dst_f, dst_rows).then_inc(dst_cast, 1)
            pool.wait_ge(dst_cast, 1)
            nc.gpsimd.tensor_tensor(rel_rows, dst_f, dst_f[:, :, 0:1].to_broadcast([GP, GQ, GROUP]), ALU.subtract).then_inc(rel_cast, 1)

            def gather(sup, k, slot_used):
                pool.wait_ge(idx_staged, sup + 1)
                if slot_used:
                    pool.wait_ge(msg_done, sup + 1 - UNROLL)
                pool.sem_inc(gather_begun, 1)
                for t in range(TILES):
                    pool.indirect_dma_start(kv[k][:, t, :], None, kv_table,
                                            bass.IndirectOffsetOnAxis(idx_slot[k][:, t:t + 1], 0)).then_inc(kv_gathered[k], 16)

            for s in range(2):
                pool.wait_ge(table_stored[s], 64 * (NCHUNK // 2))
            for k in range(UNROLL):
                gather(k, k, False)
            with pool.If(any_outside(pool) < 1):
                with pool.Fori(1, NITER) as i:
                    for k in range(UNROLL):
                        gather(UNROLL * i + k, k, True)
            with pool.Else():
                for k in range(UNROLL):
                    pool.wait_ge(kv_gathered[k], 16 * TILES)
                with pool.Fori(0, NSUPER) as sup:
                    pool.wait_ge(dst_staged, sup + 1)
                    pool.sem_inc(gather_begun, 1)
                    for t in range(TILES):
                        pool.indirect_dma_start(kv[0][:, t, :], None, kv_table,
                                                bass.IndirectOffsetOnAxis(idx_slot[0][:, t:t + 1], 0)).then_inc(kv_gathered[0], 16)
                        pool.indirect_dma_start(q_rows[:, t, :], None, q_table,
                                                bass.IndirectOffsetOnAxis(q_idx[:, t:t + 1], 0)).then_inc(q_gathered, 16)

        @block.scalar
        def _(act):
            for k, b in enumerate((bK, bV, bQ, bE)):
                act.dma_start(b_all[:, k * F:(k + 1) * F], b.rearrange("(o f) -> o f", o=1).to_broadcast([3, F])).then_inc(bias_loaded, 16)
            act.wait_ge(dve_const, 1)

            def square(c, s, slot_used):
                act.wait_ge(centred_done, c + 1)
                if slot_used:
                    act.wait_ge(sq_summed, c - 1)
                nc.scalar.activation(squared[s][:], centred[:, bass.ds(c * CF, CF)], ACT.Square).then_inc(squared_done, 1)

            def root(c):
                act.wait_ge(sq_summed, c + 1)
                cols = bass.ds(c * CT, CT)
                nc.scalar.activation(std[:, cols], sq_sum[:, cols], ACT.Sqrt, scale=1.0 / F, bias=eps_col[0:NP, :]).then_inc(std_done, 1)

            def keep_hT(c, s, slot_used):
                act.wait_ge(hT_done, c + 1)
                if slot_used:
                    act.wait_ge(rows_done, PAIRS * (c - 1))
                nc.scalar.copy(hT_sb[:, s, :, :], hT_ps[:, :, 0:NP]).then_inc(hT_copied, 1)

            def keep_rows(c, s, stores):
                if stores is not None:
                    act.wait_ge(table_stored[s], 64 * stores)
                for a in range(PAIRS):
                    act.wait_ge(rows_done, PAIRS * c + a + 1)
                    nc.scalar.copy(rows_sb[:, s, 2 * a:2 * a + 2, :].rearrange("p t f -> p (t f)"),
                                   node_ps[a][0:NP, 0:6 * F]).then_inc(rows_copied, 1)

            for c in range(6):
                square(c, c % 2, c >= 2)
                if c >= 1:
                    root(c - 1)
                if c >= 2:
                    keep_hT(c - 2, c % 2, c >= 4)
                if c >= 3:
                    keep_rows(c - 3, 1 - c % 2, (c - 3) // 2 or None)
            with act.Fori(3, NCHUNK // 2) as i:
                for s in range(2):
                    c = 2 * i + s
                    square(c, s, True)
                    root(c - 1)
                    keep_hT(c - 2, s, True)
                    keep_rows(c - 3, 1 - s, i - 2 + s)
            root(NCHUNK - 1)
            keep_hT(NCHUNK - 2, 0, True)
            keep_rows(NCHUNK - 3, 1, (NCHUNK - 3) // 2)
            keep_hT(NCHUNK - 1, 1, True)
            for c in (NCHUNK - 2, NCHUNK - 1):
                keep_rows(c, c % 2, c // 2)

            def turned(sup, k, slot_used):
                act.wait_ge(attrT_done, sup + 1)
                if slot_used:
                    act.wait_ge(e_done, sup - 1)
                nc.scalar.copy(attrT[k % 2][:], attrT_ps).then_inc(attrT_copied, 1)
                act.wait_ge(onehotT_done, sup + 1)
                if slot_used:
                    act.wait_ge(qe_done, sup - 1)
                nc.scalar.copy(onehotT[k % 2][:], onehotT_ps).then_inc(onehotT_copied, 1)

            def weights(sup, first):
                act.wait_ge(clip_done, sup + 1)
                if not first:
                    act.wait_ge(msg_done, sup)
                nc.scalar.activation(weight[:], clipped[:], ACT.Exp).then_inc(weight_done, 1)

            with act.If(any_outside(act) < 1):
                for k in range(UNROLL):
                    turned(k, k, k >= 2)
                    if k > 0:
                        weights(k - 1, k == 1)
                with act.Fori(1, NITER) as i:
                    for k in range(UNROLL):
                        turned(UNROLL * i + k, k, True)
                        weights(UNROLL * i + k - 1, False)
                weights(NSUPER - 1, False)
            with act.Else():
                with act.Fori(0, NSUPER) as sup:
                    act.wait_ge(attrT_done, sup + 1)
                    nc.scalar.copy(attrT[0][:], attrT_ps).then_inc(attrT_copied, 1)
                    act.wait_ge(clip_done, sup + 1)
                    nc.scalar.activation(weight[:], clipped[:], ACT.Exp).then_inc(weight_done, 1)

        @block.vector
        def _(dve):
            nc.vector.memset(eps_col[:], EPS).then_inc(dve_const, 1)
            nc.vector.memset(ones3[:], 1.0).then_inc(dve_const, 1)
            nc.vector.memset(ones_col[:], 1.0).then_inc(dve_const, 1)
            def split(ins):
                split.steps += 1
                ins.then_inc(split_step, 1)
                dve.wait_ge(split_step, split.steps)

            def split_biases():
                split.steps = 0
                dve.wait_ge(bias_loaded, 64)
                dve.wait_ge(pool_const, 2)
                split(nc.vector.tensor_copy(b_part[0][:], b_all[:]))
                split(nc.vector.tensor_tensor(b_rest[:], b_all[:], b_part[0][:], ALU.subtract))
                split(nc.vector.tensor_copy(b_part[1][:], b_rest[:]))
                split(nc.vector.tensor_tensor(b_part[2][:], b_rest[:], b_part[1][:], ALU.subtract))
                split(nc.vector.tensor_scalar(b3[:], b_part[0][:], ident[0:3, 0:1], None, ALU.mult))
                split(nc.vector.scalar_tensor_tensor(out=b_pick[:], in0=b_part[1][:], scalar=ident[0:3, 1:2], in1=b3[:], op0=ALU.mult, op1=ALU.add))
                split(nc.vector.scalar_tensor_tensor(out=b3[:], in0=b_part[2][:], scalar=ident[0:3, 2:3], in1=b_pick[:], op0=ALU.mult, op1=ALU.add))
                for t in range(2):
                    nc.vector.tensor_copy(b3_node[:, t, :], b3[:, 0:3 * F])
                nc.vector.tensor_copy(b3_edge[:], b3[:, None, 3 * F:].to_broadcast([3, TILES, F])).then_inc(bias_spread, 1)

            def rows_of(a, c):
                return a[:, bass.ds(c * CF, CF)].rearrange("p (t f) -> p t f", f=F)

            def centre(c):
                cols = bass.ds(c * CT, CT)
                nc.vector.tensor_reduce(row_sum[:, cols], rows_of(x_sb, c), AX.X, ALU.add).then_inc(summed, 1)
                dve.wait_ge(summed, c + 1)
                nc.vector.scalar_tensor_tensor(
                    out=rows_of(centred, c), in0=row_sum[:, cols][:, :, None].to_broadcast([NP, CT, F]), scalar=-1.0 / F,
                    in1=rows_of(x_sb, c), op0=ALU.mult, op1=ALU.add).then_inc(centred_done, 1)

            def sum_squares(c, s):
                dve.wait_ge(squared_done, c + 1)
                nc.vector.tensor_reduce(sq_sum[:, bass.ds(c * CT, CT)], squared[s].rearrange("p (t f) -> p t f", f=F),
                                        AX.X, ALU.add).then_inc(sq_summed, 1)

            def scale(c, s, slot_used):
                cols = bass.ds(c * CT, CT)
                dve.wait_ge(std_done, c + 1)
                nc.vector.reciprocal(rstd[:, cols], std[:, cols]).then_inc(rstd_done, 1)
                dve.wait_ge(rstd_done, c + 1)
                if slot_used:
                    dve.wait_ge(hT_done, c - 1)
                nc.vector.scalar_tensor_tensor(
                    out=h_sb[s].rearrange("p (t f) -> p t f", f=F), in0=rows_of(centred, c), scalar=0.0,
                    in1=rstd[:, cols][:, :, None].to_broadcast([NP, CT, F]), op0=ALU.max, op1=ALU.mult).then_inc(h_done, 1)

            dve.wait_ge(x_loaded[0], 32)
            centre(0)
            centre(1)
            sum_squares(0, 0)
            split_biases()
            dve.wait_ge(x_loaded[1], 32)
            for c in (2, 3):
                centre(c)
                sum_squares(c - 1, 1 - c % 2)
                scale(c - 2, c % 2, False)
            dve.wait_ge(x_loaded[2], 32)
            with dve.Fori(2, NCHUNK // 2) as i:
                for s in range(2):
                    c = 2 * i + s
                    centre(c)
                    sum_squares(c - 1, 1 - s)
                    scale(c - 2, s, True)
            sum_squares(NCHUNK - 1, 1)
            for s in range(2):
                scale(NCHUNK - 2 + s, s, True)

            def keep_index(kept, turn, q):
                dve.wait_ge(idx_turned, turn + 1)
                nc.vector.tensor_copy(kept[:, q * GP:(q + 1) * GP, :].rearrange("p r g -> p g r"),
                                      idx_ps[turn % 2][:, 0:G * GP].rearrange("p (g r) -> p g r", g=G)).then_inc(idx_kept, 1)

            def stage_idx(sup, k):
                nc.vector.tensor_copy(idx_slot[k][:].rearrange("p (g h) -> p h g", g=G),
                                      src_idx[:, bass.ds(HALVES * sup, HALVES), :]).then_inc(idx_staged, 1)

            for q in range(GQ):
                keep_index(src_idx, q, q)
            dve.wait_ge(pool_const, 2)
            dve.wait_ge(idx_kept, GQ)
            for k in range(UNROLL):
                stage_idx(k, k)
            for q in range(GQ):
                keep_index(dst_rel, GQ + q, q)
            dve.wait_ge(idx_kept, 2 * GQ)
            all_rel = dst_rel[:].rearrange("p j g -> p (j g)")
            nc.vector.tensor_reduce(lowest[:], all_rel, AX.X, ALU.min).then_inc(bounds_found, 1)
            nc.vector.tensor_reduce(highest[:], all_rel, AX.X, ALU.max).then_inc(bounds_found, 1)
            dve.wait_ge(bounds_found, 2)
            nc.vector.tensor_scalar(highest[:], highest[:], float(WINDOW), None, ALU.is_ge).then_inc(bounds_found, 1)
            dve.wait_ge(bounds_found, 3)
            nc.vector.scalar_tensor_tensor(out=outside[:], in0=lowest[:], scalar=0.0, in1=highest[:],
                                           op0=ALU.is_lt, op1=ALU.add).then_inc(outside_found, 1)
            nc.vector.memset(dst_rel[0:OVERLAP // G, FULL, :], -1.0).then_inc(masked, 1)
            nc.vector.memset(acc[:], 0.0).then_inc(acc_zeroed, 1)
            dve.wait_ge(masked, 1)
            dve.wait_ge(acc_zeroed, 1)

            def build_onehot(sup, k, slot_used):
                if slot_used:
                    dve.wait_ge(sums_done, sup - UNROLL + 1)
                nc.vector.tensor_tensor(
                    onehot[k][:],
                    iota_w[:, None, None, :].to_broadcast([P, G, HALVES, WINDOW]),
                    dst_rel[:, bass.ds(HALVES * sup, HALVES), :].rearrange("p h g -> p g h")[:, :, :, None].to_broadcast([P, G, HALVES, WINDOW]),
                    ALU.is_equal).then_inc(onehot_built, 1)

            def messages(sup, rounds, k):
                s = k % 2
                dve.wait_ge(kv_gathered[k], 16 * TILES * rounds)
                stage_idx(sup + UNROLL, k)
                dve.wait_ge(e_done, sup + 1)
                nc.vector.tensor_tensor(prod[:], kv[k][:, :, 0:F], e_ps[s].rearrange("p (t f) -> p t f", f=F),
                                        ALU.mult).then_inc(ke_done, 1)
                dve.wait_ge(qe_done, sup + 1)
                weigh(sup, kv[k], qe_ps[s][:], msg[s])

            def weigh(sup, rows, q, messages_out):
                dve.wait_ge(ke_done, sup + 1)
                nc.vector.scalar_tensor_tensor(
                    out=prod[:].rearrange("p t f -> p (t f)"), in0=prod[:].rearrange("p t f -> p (t f)"),
                    scalar=INV_SQRT_D, in1=q, op0=ALU.mult, op1=ALU.mult).then_inc(keq_done, 1)
                dve.wait_ge(keq_done, sup + 1)
                nc.vector.tensor_reduce(logits[:], prod[:].rearrange("p t (h d) -> p t h d", d=D), AX.X, ALU.add).then_inc(logits_done, 1)
                dve.wait_ge(logits_done, sup + 1)
                nc.vector.tensor_scalar(clipped[:], logits[:], CLIP, -CLIP, ALU.min, ALU.max).then_inc(clip_done, 1)
                dve.wait_ge(weight_done, sup + 1)
                nc.vector.tensor_tensor(
                    messages_out.rearrange("p g h (a d) -> p (g h) a d", d=D),
                    rows[:, :, F:].rearrange("p t (a d) -> p t a d", d=D),
                    weight[:, :, :, None].to_broadcast([P, TILES, H, D]), ALU.mult).then_inc(msg_done, 1)

            def add_sums(sup, first):
                base = [dve.value_load(base_i[0:1, bass.ds(HALVES * sup + h, 1)], min_val=0, max_val=N - 1) for h in range(HALVES)]
                dve.wait_ge(sums_done, sup + 1)
                if not first:
                    dve.wait_ge(added, HALVES * sup)
                for half in range(HALVES):
                    rows = slice(half * F, (half + 1) * F)
                    win = acc[rows, bass.ds(base[half], WINDOW)]
                    nc.vector.tensor_tensor(win, win, sum_ps[rows, half * WINDOW:(half + 1) * WINDOW], ALU.add).then_inc(added, 1)

            dve.wait_ge(base_loaded, 32)
            dve.wait_ge(outside_counted, 1)
            nc.vector.tensor_copy(scattered[:], base_ps[0:1, 0:1]).then_inc(form_known, 1)
            with dve.If(any_outside(dve) < 1):
                for k in range(UNROLL):
                    build_onehot(k, k, False)
                    if k > 0:
                        messages(k - 1, 1, k - 1)
                    if k > 1:
                        add_sums(k - 2, k == 2)
                with dve.Fori(1, NITER) as i:
                    for k in range(UNROLL):
                        sup = UNROLL * i + k
                        build_onehot(sup, k, True)
                        messages(sup - 1, i + 1 if k else i, (k - 1) % UNROLL)
                        add_sums(sup - 2, False)
                messages(NSUPER - 1, NITER, UNROLL - 1)
                add_sums(NSUPER - 2, False)
                add_sums(NSUPER - 1, False)
                dve.wait_ge(added, HALVES * NSUPER)
                dve.sem_inc(edges_summed, 1)
            with dve.Else():
                nc.vector.tensor_copy(base_f[:], base_i[:]).then_inc(base_cast, 1)
                nc.vector.memset(ones_row[:], 1.0).then_inc(base_cast, 1)
                dve.wait_ge(base_spread, 1)
                nc.vector.tensor_tensor(dst_rel[:], dst_rel[:], base_ps[:, 0:NGROUP, None].to_broadcast([P, NGROUP, G]),
                                        ALU.add).then_inc(dst_restored, 1)
                dve.wait_ge(dst_restored, 1)
                nc.vector.memset(dst_rel[0:OVERLAP // G, FULL, :], -1.0).then_inc(dst_restored, 1)
                dve.wait_ge(dst_restored, 2)
                for k in range(UNROLL):
                    dve.wait_ge(kv_gathered[k], 16 * TILES)
                with dve.Fori(0, NSUPER) as sup:
                    nc.vector.tensor_copy(idx_slot[0][:].rearrange("p (g h) -> p h g", g=G), src_idx[:, bass.ds(HALVES * sup, HALVES), :])
                    nc.vector.tensor_copy(dst_now[:].rearrange("p (g h) -> p h g", g=G), dst_rel[:, bass.ds(HALVES * sup, HALVES), :])
                    nc.vector.tensor_scalar(q_idx[:].rearrange("p (g h) -> p h g", g=G), dst_rel[:, bass.ds(HALVES * sup, HALVES), :],
                                            0.0, None, ALU.max).then_inc(dst_staged, 1)
                    dve.wait_ge(kv_gathered[0], 16 * TILES * (sup + 2))
                    dve.wait_ge(q_gathered, 16 * TILES * (sup + 1))
                    dve.wait_ge(e_done, sup + 1)
                    nc.vector.tensor_tensor(prod[:], kv[0][:, :, 0:F], e_ps[0].rearrange("p (t f) -> p t f", f=F),
                                            ALU.mult).then_inc(ke_done, 1)
                    weigh(sup, kv[0], q_rows.rearrange("p t f -> p (t f)"), msg[0])
                    with dve.Fori(0, NWINDOW) as w:
                        turn = sup * NWINDOW + w
                        nc.vector.scalar_tensor_tensor(
                            out=onehot[0].rearrange("p g h w -> p (g h) w"),
                            in0=dst_now[:, :, None].to_broadcast([P, TILES, WINDOW]), scalar=win_start[:, bass.ds(w, 1)],
                            in1=iota_w[:, None, :].to_broadcast([P, TILES, WINDOW]),
                            op0=ALU.subtract, op1=ALU.is_equal).then_inc(onehot_built, 1)
                        dve.wait_ge(sums_done, turn + 1)
                        for half in range(HALVES):
                            rows = slice(half * F, (half + 1) * F)
                            win = acc[rows, bass.ds(w * WINDOW, WINDOW)]
                            nc.vector.tensor_tensor(win, win, sum_ps[rows, half * WINDOW:(half + 1) * WINDOW], ALU.add).then_inc(added, 1)
                        dve.wait_ge(added, HALVES * (turn + 1))
                dve.sem_inc(edges_summed, 1)

            for c, (t, end) in enumerate(OUT_STEPS):
                dve.wait_ge(out_turned, c + 1)
                rows = x_sb[:, t * F:end * F].rearrange("p (t f) -> p t f", f=F)
                sums = wide[c % 2][0:NP, 0:(end - t) * P].rearrange("p (t h f) -> p t h f", h=HALVES, f=F)
                for half in range(HALVES):
                    if half:
                        dve.wait_ge(out_added, HALVES * c + half)
                    nc.vector.tensor_tensor(rows, rows, sums[:, :, half, :], ALU.add).then_inc(out_added, 1)

        @block.tensor
        def _(pe):
            pe.wait_ge(pool_const, 2)
            pe.wait_ge(dve_const, 3)
            def turn_h(c, s, bank_used):
                pe.wait_ge(h_done, c + 1)
                if bank_used:
                    pe.wait_ge(hT_copied, c)
                for a in range(PAIRS):
                    last = nc.tensor.transpose(hT_ps[:, a, 0:NP], h_sb[s][:, 2 * a * F:2 * (a + 1) * F], ident[0:NP, 0:NP])
                last.then_inc(hT_done, 1)

            def project_h(c, s, banks_used):
                pe.wait_ge(hT_copied, c + 1)
                for a in range(PAIRS):
                    if banks_used:
                        pe.wait_ge(rows_copied, PAIRS * (c - 1) + a + 1)
                    rows = node_ps[a][0:NP, 0:6 * F]
                    nc.tensor.matmul(rows, ones3[:, 0:NP], b3_node[:].rearrange("k t f -> k (t f)"), start=True, stop=False)
                    nc.tensor.matmul(rows, hT_sb[:, s, a, :], w_node[:].rearrange("k t f -> k (t f)"), start=False, stop=True).then_inc(rows_done, 1)

            turn_h(0, 0, False)
            turn_h(1, 1, True)
            pe.wait_ge(bias_spread, 1)
            pe.wait_ge(weights_loaded, 16 * 6)
            project_h(0, 0, False)
            with pe.Fori(1, NCHUNK // 2) as i:
                for s in range(2):
                    c = 2 * i + s
                    turn_h(c, s, True)
                    project_h(c - 1, 1 - s, True)
            project_h(NCHUNK - 1, 1, True)

            for n, (rows, cast) in enumerate(((src_f, idx_cast), (rel_rows, rel_cast))):
                pe.wait_ge(cast, 1)
                for q in range(GQ):
                    turn = n * GQ + q
                    if turn >= 2:
                        pe.wait_ge(idx_kept, turn - 1)
                    for g in range(G):
                        last = nc.tensor.transpose(idx_ps[turn % 2][:, g * GP:(g + 1) * GP],
                                                   rows[:, q, :].rearrange("r (p g) -> r g p", g=G)[:, g, :], ident[0:GP, 0:GP])
                    last.then_inc(idx_turned, 1)
            pe.wait_ge(outside_found, 1)
            pe.wait_ge(idx_kept, 2 * GQ)
            nc.tensor.matmul(base_ps[0:1, 0:1], outside[:], ones_col[:], start=True, stop=True).then_inc(outside_counted, 1)
            pe.wait_ge(rows_copied, PAIRS * NCHUNK)
            pe.wait_ge(edge_weights_loaded, 32)

            def turn_features(s):
                for g in range(G):
                    last = nc.tensor.transpose(attrT_ps[:, g, :], attr[s].rearrange("p h g f -> p (h g f)")[:, 2 * g * F:2 * (g + 1) * F], ident[:])
                last.then_inc(attrT_done, 1)

            def project_features(s):
                nc.tensor.matmul(e_ps[s][:], ones3[:, :], b3_edge[:].rearrange("k t f -> k (t f)"), start=True, stop=False)
                for a in range(G):
                    half, pair = a // 2, a % 2
                    last = nc.tensor.matmul(
                        e_ps[s].rearrange("p (g h f) -> p h g f", g=G, h=HALVES)[:, half, 2 * pair:2 * pair + 2, :],
                        attrT[s][:, a, :], w_edge[:], start=False, stop=a == G - 1)
                last.then_inc(e_done, 1)

            def sum_by_node(messages, hot):
                for g in range(G):
                    last = nc.tensor.matmul(sum_ps[:, 0:HALVES * WINDOW], messages[:, g, :, :].rearrange("p h f -> p (h f)"),
                                            hot[:, g, :, :].rearrange("p h w -> p (h w)"), start=g == 0, stop=g == G - 1)
                last.then_inc(sums_done, 1)

            def expand(i, k, first):
                sup = UNROLL * i + k
                s = k % 2
                pe.wait_ge(attr_loaded[s], 16 * (UNROLL // 2 * i + k // 2 + 1))
                if not first or k > 0:
                    pe.wait_ge(attrT_copied, sup)
                turn_features(s)
                pe.wait_ge(onehot_built, sup + 1)
                if not first or k > 0:
                    pe.wait_ge(onehotT_copied, sup)
                for g in range(G):
                    last = nc.tensor.transpose(onehotT_ps[:, g, :], onehot[k][:, g, :, :].rearrange("p h w -> p (h w)"), ident[:])
                last.then_inc(onehotT_done, 1)
                pe.wait_ge(attrT_copied, sup + 1)
                if not first or k >= 2:
                    pe.wait_ge(ke_done, sup - 1)
                project_features(s)
                pe.wait_ge(onehotT_copied, sup + 1)
                pe.wait_ge(q_loaded[s], 32 * (UNROLL // 2 * i + k // 2 + 1))
                if not first or k >= 2:
                    pe.wait_ge(keq_done, sup - 1)
                for g in range(G):
                    last = nc.tensor.matmul(qe_ps[s][:, 2 * g * F:2 * (g + 1) * F],
                                            onehotT[s][:, g, :], q_win[s].rearrange("k h f -> k (h f)"), start=True, stop=True)
                last.then_inc(qe_done, 1)

            def sum_messages(sup, k, first):
                pe.wait_ge(msg_done, sup + 1)
                if not first:
                    pe.wait_ge(added, HALVES * sup)
                sum_by_node(msg[k % 2], onehot[k])

            with pe.If(any_outside(pe) < 1):
                for k in range(UNROLL):
                    expand(0, k, True)
                    if k > 0:
                        sum_messages(k - 1, k - 1, k == 1)
                with pe.Fori(1, NITER) as i:
                    for k in range(UNROLL):
                        expand(i, k, False)
                        sum_messages(UNROLL * i + k - 1, (k - 1) % UNROLL, False)
                sum_messages(NSUPER - 1, UNROLL - 1, False)
            with pe.Else():
                pe.wait_ge(base_cast, 2)
                nc.tensor.matmul(base_ps[:, 0:NGROUP], ones_row[:], base_f[:], start=True, stop=True).then_inc(base_spread, 1)
                with pe.Fori(0, NSUPER) as sup:
                    pe.wait_ge(attr_loaded[0], 16 * (sup + 1))
                    turn_features(0)
                    pe.wait_ge(attrT_copied, sup + 1)
                    pe.wait_ge(dst_staged, sup + 1)
                    project_features(0)
                    with pe.Fori(0, NWINDOW) as w:
                        pe.wait_ge(msg_done, sup + 1)
                        pe.wait_ge(onehot_built, sup * NWINDOW + w + 1)
                        sum_by_node(msg[0], onehot[0])

            pe.wait_ge(edges_summed, 1)
            acc_nodes = acc[:, 0:N].rearrange("p (n t) -> p t n", t=NPP)
            for c, (t, end) in enumerate(OUT_STEPS):
                if c >= 2:
                    pe.wait_ge(out_added, HALVES * (c - 1))
                for k in range(end - t):
                    last = nc.tensor.transpose(wide[c % 2][0:NP, k * P:(k + 1) * P], acc_nodes[:, t + k, :], ident[:])
                last.then_inc(out_turned, 1)


_INS = ["x", "src", "dst", "edge_attr_64", "L0_gnn_WQ", "L0_gnn_bQ", "L0_gnn_WK", "L0_gnn_bK",
        "L0_gnn_WE", "L0_gnn_bE", "L0_gnn_WV", "L0_gnn_bV"]


def kernel(**inputs):
    import concourse.bacc as _bacc
    from concourse.bass_utils import run_bass_kernel_spmd as _run

    nc = _bacc.Bacc("TRN2", target_bir_lowering=False, num_devices=1)
    arrays, args = {}, []
    for name in _INS:
        a = np.ascontiguousarray(inputs[name])
        arrays[f"in_{name}"] = a
        args.append(nc.dram_tensor(f"in_{name}", a.shape, mybir.dt.from_np(a.dtype), kind="ExternalInput").ap())
    out = nc.dram_tensor("out_0", (N, F), FP32, kind="ExternalOutput").ap()
    build(nc, *args, out)
    r = _run(nc, [arrays], core_ids=[0])
    return r.results[0]["out_0"]
```

```python
from contextlib import ExitStack

import numpy as np
import concourse.bass as bass
from concourse import mybir

FP32, BF16 = mybir.dt.float32, mybir.dt.bfloat16
I32, U32 = mybir.dt.int32, mybir.dt.uint32
ALU = mybir.AluOpType
ACT = mybir.ActivationFunctionType
AX = mybir.AxisListType

N, F, E = 12500, 64, 212500
H = 8
D = F // H
P = 128
EPS = 1e-5
CLIP = 5.0
INV_SQRT_D = float(np.float32(1.0 / np.sqrt(D)))

NP, NPP = 125, 100
CT = 10
NCHUNK = NPP // CT
PAIRS = CT // 2
CF = CT * F
OUT_ENDS = [8, 24, 40, 56, 72, 88, 96, NPP]
OUT_STEPS = list(zip([0] + OUT_ENDS, OUT_ENDS))
X_LOADS = [(0, 2), (2, 4), (4, 6), (6, NCHUNK)]
CUTS = [(0, 112), (112, NP)]

G = 4
GROUP = P * G
HALVES = 2
TILES = HALVES * G
SUPER = HALVES * GROUP
NSUPER = -(-E // SUPER)
TAIL = E - SUPER
OVERLAP = (NSUPER - 1) * SUPER - TAIL
NGROUP = NSUPER * HALVES
FULL = NGROUP - HALVES
GP = 104
GQ = NGROUP // GP
WINDOW = 64
NWINDOW = -(-N // WINDOW)
UNROLL = 4
EARLY = UNROLL - 1
NITER = NSUPER // UNROLL
assert GP * GQ == NGROUP and NITER * UNROLL == NSUPER and OVERLAP % G == 0
assert NP * NPP == N and NCHUNK * CT == NPP and NCHUNK % 2 == 0
assert NCHUNK // 2 - 1 == GQ


def build(nc, x, src, dst, edge_attr, WQ, bQ, WK, bK, WE, bE, WV, bV, out):
    kv_table = nc.dram_tensor("kv_table", (N, 2 * F), FP32).ap()
    q_table = nc.dram_tensor("q_table", (N + WINDOW, F), FP32).ap()

    ctx = ExitStack()
    with ctx:
        def sb(name, shape, dt=FP32):
            return ctx.enter_context(nc.sbuf_tensor(name, shape, dt))

        def sem(name):
            return ctx.enter_context(nc.semaphore(name))

        def sems(name, n):
            return [sem(f"{name}{k}") for k in range(n)]

        ident = sb("ident", [P, P])
        iota_i = sb("iota_i", [P, WINDOW], I32)
        iota_w = sb("iota_w", [P, WINDOW])
        ones3 = sb("ones3", [3, P], BF16)
        ones_col = sb("ones_col", [P, 1])
        zeros = sb("zeros", [WINDOW, F])
        eps_col = sb("eps_col", [P, 1])
        zero_col, warm_col = sb("zero_col", [P, 1]), sb("warm_col", [P, 1])
        w_node = sb("w_node", [P, 2, 3 * F])
        w_edge = sb("w_edge", [P, 2, F])
        NB = 3 * F + F
        b_all = sb("b_all", [3, NB])
        b_rest = sb("b_rest", [3, NB])
        b_part = [sb(f"b_part{k}", [3, NB], BF16) for k in range(3)]
        b_pick = sb("b_pick", [3, NB], BF16)
        b3 = sb("b3", [3, NB], BF16)
        x_sb = sb("x_sb", [NP, NPP * F])
        row_sum = sb("row_sum", [NP, NPP])
        centred_all = sb("centred_all", [P, NPP * F])
        centred = centred_all[0:NP, :]
        squared = [sb(f"squared{k}", [NP, CF]) for k in range(2)]
        sq_sum = sb("sq_sum", [NP, NPP])
        std = sb("std", [NP, NPP])
        rstd = sb("rstd", [NP, NPP])
        h_sb = [sb(f"h_sb{k}", [NP, CF]) for k in range(2)]
        hT_sb = sb("hT_sb", [P, 2, PAIRS, NP])
        kv_out = sb("kv_out", [NP, 2, CT, 2 * F])
        q_out = sb("q_out", [NP, 2, CT, F])
        acc = sb("acc", [P, N + WINDOW])
        RW = GQ * GROUP
        src_rows, dst_rows = (acc[0:GP, k * RW:(k + 1) * RW].bitcast(I32).rearrange("r (q e) -> r q e", q=GQ) for k in range(2))
        dst_f, src_f, rel_rows = (acc[0:GP, k * RW:(k + 1) * RW].rearrange("r (q e) -> r q e", q=GQ) for k in range(2, 5))
        base_i = sb("base_i", [1, NGROUP], I32)
        src_idx = sb("src_idx", [P, NGROUP + HALVES * UNROLL, G], U32)
        dst_rel = sb("dst_rel", [P, NGROUP, G])
        lows, highs = sb("lows", [P, GQ]), sb("highs", [P, GQ])
        lowest, highest = sb("lowest", [P, 1]), sb("highest", [P, 1])
        outside = sb("outside", [P, 1])
        scattered = sb("scattered", [1, 1], I32)
        base_f = sb("base_f", [1, NGROUP])
        ones_row = sb("ones_row", [1, P])
        win_i = sb("win_i", [P, NWINDOW], I32)
        win_start = sb("win_start", [P, NWINDOW])
        dst_now = sb("dst_now", [P, TILES])
        q_idx = sb("q_idx", [P, TILES], U32)
        idx_slot = [sb(f"idx_slot{k}", [P, TILES], U32) for k in range(UNROLL + EARLY)]
        kv = [sb(f"kv{k}", [P, TILES, 2 * F]) for k in range(UNROLL)]
        SLOT = TILES * 2 * F
        kv += [centred_all[:, k * SLOT:(k + 1) * SLOT].rearrange("p (t f) -> p t f", t=TILES) for k in range(EARLY)]
        attr = [sb(f"attr{k}", [P, HALVES, G, F]) for k in range(2)]
        attrT = [sb(f"attrT{k}", [P, G, P]) for k in range(2)]
        onehot = [sb(f"onehot{k}", [P, G, HALVES, WINDOW]) for k in range(UNROLL)]
        onehotT = [sb(f"onehotT{k}", [P, G, P]) for k in range(2)]
        q_win = [sb(f"q_win{k}", [P, HALVES, F]) for k in range(2)]
        prod = sb("prod", [P, TILES, F])
        logits = sb("logits", [P, TILES, H])
        clipped = sb("clipped", [P, TILES, H])
        weight = sb("weight", [P, TILES, H])
        msg = [sb(f"msg{k}", [P, G, HALVES, F]) for k in range(2)]

        wide = [ctx.enter_context(nc.psum_tensor(f"wide{k}", [P, 1024], FP32)) for k in range(2)]
        bank = [ctx.enter_context(nc.psum_tensor(f"bank{k}", [P, 512], FP32))[:] for k in range(4)]
        hT_ps = wide[0][:, 0:PAIRS * P].rearrange("p (a n) -> p a n", n=P)
        node_ps = bank + [wide[1][:, 0:512]]
        idx_ps = [wide[1][:, 512:1024], wide[0][:, 0:512]]
        attrT_ps = wide[0][:, 0:512].rearrange("p (a n) -> p a n", n=P)
        onehotT_ps = wide[0][:, 512:1024].rearrange("p (a n) -> p a n", n=P)
        e_ps = bank[0:2]
        qe_ps = bank[2:4]
        sum_ps = wide[1][:, 0:512]
        base_ps = wide[1][:, 512:1024]

        zeroed, weights_loaded, edge_weights_loaded, bias_loaded = (
            sem(n) for n in ("zeroed", "weights_loaded", "edge_weights_loaded", "bias_loaded"))
        pool_const, dve_const, table_warm = sem("pool_const"), sem("dve_const"), sem("table_warm")
        split_step, bias_split = sem("split_step"), sem("bias_split")
        pad_stored = sem("pad_stored")
        x_loaded = sems("x_loaded", len(X_LOADS))
        summed, centred_done, squared_done, sq_summed = (sem(n) for n in ("summed", "centred_done", "squared_done", "sq_summed"))
        std_done, rstd_done, h_done, h_again = (sem(n) for n in ("std_done", "rstd_done", "h_done", "h_again"))
        hT_done, hT_copied, rows_done, rows_copied = (sem(n) for n in ("hT_done", "hT_copied", "rows_done", "rows_copied"))
        kv_stored, q_stored = sems("kv_stored", 2), sems("q_stored", 2)
        src_loaded, dst_loaded, base_loaded = sem("src_loaded"), sem("dst_loaded"), sem("base_loaded")
        src_cast, dst_cast, rel_cast = sem("src_cast"), sem("dst_cast"), sem("rel_cast")
        idx_turned, idx_kept, masked = sem("idx_turned"), sem("idx_kept"), sem("masked")
        attr_loaded, q_loaded = sems("attr_loaded", 2), sems("q_loaded", 2)
        gather_begun, kv_gathered = sem("gather_begun"), sems("kv_gathered", UNROLL + EARLY)
        idx_staged, onehot_built, ke_done, keq_done = (sem(n) for n in ("idx_staged", "onehot_built", "ke_done", "keq_done"))
        logits_done, clip_done, weight_done, msg_done, added = (sem(n) for n in ("logits_done", "clip_done", "weight_done", "msg_done", "added"))
        attrT_done, attrT_copied, onehotT_done, onehotT_copied = (sem(n) for n in ("attrT_done", "attrT_copied", "onehotT_done", "onehotT_copied"))
        e_done, qe_done, sums_done = sem("e_done"), sem("qe_done"), sem("sums_done")
        acc_zeroed = sem("acc_zeroed")
        part_bounded = sem("part_bounded")
        bounds_found, outside_found, outside_counted, form_known = (sem(n) for n in ("bounds_found", "outside_found", "outside_counted", "form_known"))
        base_cast, base_spread, dst_restored, dst_staged, q_gathered = (sem(n) for n in ("base_cast", "base_spread", "dst_restored", "dst_staged", "q_gathered"))
        edges_summed = sem("edges_summed")
        out_turned, out_added, out_stored = sem("out_turned"), sem("out_added"), sem("out_stored")

        def load_rows(eng, rows, arr, loaded):
            lead = (GQ - 1) * GP
            eng.dma_start(rows[:, 0:GQ - 1, :], arr[0:lead * GROUP].rearrange("(q r e) -> r q e", r=GP, e=GROUP)).then_inc(loaded, 16)
            eng.dma_start(rows[0:FULL - lead, GQ - 1, :], arr[lead * GROUP:FULL * GROUP].rearrange("(r e) -> r e", e=GROUP)).then_inc(loaded, 16)
            eng.dma_start(rows[FULL - lead:GP, GQ - 1, :], arr[TAIL:E].rearrange("(r e) -> r e", e=GROUP)).then_inc(loaded, 16)

        def any_outside(eng):
            eng.wait_ge(form_known, 1)
            return eng.value_load(scattered[0:1, 0:1], min_val=0, max_val=2 * P)

        q_rows = kv[1][:].rearrange("p t f -> p (t f)")[:, 0:TILES * F].rearrange("p (t f) -> p t f", f=F)
        x_v = x.rearrange("(p t) f -> p (t f)", p=NP)
        out_v = out.rearrange("(p t) f -> p (t f)", p=NP)
        kv_v = kv_table.rearrange("(p t) f -> p t f", p=NP)
        q_v = q_table[0:N, :].rearrange("(p t) f -> p t f", p=NP)

        block = ctx.enter_context(nc.Block())

        @block.sync
        def _(sp):
            for n, (c, end) in enumerate(X_LOADS):
                if n == len(X_LOADS) - 1:
                    sp.wait_ge(weights_loaded, 16 * 6)
                for a, b in CUTS:
                    sp.dma_start(x_sb[a:b, c * CF:end * CF], x_v[a:b, c * CF:end * CF]).then_inc(x_loaded[n], 16)
            load_rows(sp, dst_rows, dst, dst_loaded)
            load_rows(sp, src_rows, src, src_loaded)
            with nc.allow_non_contiguous_dma("one dst of each group"):
                sp.dma_start(base_i[0:1, 0:FULL], dst[0:FULL * GROUP].rearrange("(o j e) -> o j e", o=1, e=GROUP)[:, :, 0]).then_inc(base_loaded, 16)
                sp.dma_start(base_i[0:1, FULL:NGROUP], dst[TAIL:E].rearrange("(o j e) -> o j e", o=1, e=GROUP)[:, :, 0]).then_inc(base_loaded, 16)
            sp.wait_ge(zeroed, 1)
            for blk in range(2):
                sp.dma_start(w_edge[blk * F:(blk + 1) * F, blk, :], WE).then_inc(edge_weights_loaded, 16)

            with sp.Fori(0, NCHUNK // 2) as i:
                for s in range(2):
                    c = 2 * i + s
                    sp.wait_ge(rows_copied, PAIRS * (c + 1))
                    for a, b in CUTS:
                        sp.dma_start(kv_v[a:b, bass.ds(c * CT, CT), :], kv_out[a:b, s, :, :]).then_inc(kv_stored[s], 16)

            def load_attr(first_edge, s):
                sp.dma_start(attr[s].rearrange("p h g f -> p h (g f)"),
                             edge_attr[bass.ds(first_edge, SUPER), :].rearrange("(h p g) f -> p h (g f)", h=HALVES, g=G)
                             ).then_inc(attr_loaded[s], 16)

            for s in range(2):
                load_attr(s * SUPER, s)

            with sp.Fori(0, NCHUNK // 2) as i:
                for s in range(2):
                    c = 2 * i + s
                    sp.wait_ge(rows_copied, PAIRS * (NCHUNK + c + 1))
                    for a, b in CUTS:
                        sp.dma_start(q_v[a:b, bass.ds(c * CT, CT), :], q_out[a:b, s, :, :]).then_inc(q_stored[s], 16)

            def load_q(base, s):
                for half in range(HALVES):
                    rows = slice(half * F, half * F + WINDOW)
                    sp.dma_start(q_win[s][rows, half, :], q_table[bass.ds(base[half], WINDOW), :]).then_inc(q_loaded[s], 16)

            def loads(sup, first_edge, k):
                base = [sp.value_load(base_i[0:1, bass.ds(HALVES * sup + h, 1)], min_val=0, max_val=N - 1) for h in range(HALVES)]
                sp.wait_ge(attrT_done, sup - 1)
                load_attr(first_edge, k % 2)
                sp.wait_ge(qe_done, sup - 1)
                load_q(base, k % 2)

            sp.wait_ge(base_loaded, 32)
            first_bases = [sp.value_load(base_i[0:1, g:g + 1], min_val=0, max_val=N - 1) for g in range(2 * HALVES)]
            sp.wait_ge(pad_stored, 16)
            for s in range(2):
                sp.wait_ge(q_stored[s], 32 * (NCHUNK // 2))
            for s in range(2):
                load_q(first_bases[s * HALVES:(s + 1) * HALVES], s)
            with sp.If(any_outside(sp) < 1):
                for k in range(2, UNROLL):
                    loads(k, k * SUPER, k)
                with sp.Fori(1, NITER - 1) as i:
                    for k in range(UNROLL):
                        loads(UNROLL * i + k, (UNROLL * i + k) * SUPER, k)
                for k in range(UNROLL):
                    sup = NSUPER - UNROLL + k
                    loads(sup, sup * SUPER if sup < NSUPER - 1 else TAIL, k)
            with sp.Else():
                with sp.Fori(1, NSUPER - 1) as sup:
                    sp.wait_ge(attrT_done, sup)
                    load_attr(sup * SUPER, 0)
                sp.wait_ge(attrT_done, NSUPER - 1)
                load_attr(TAIL, 0)

            for c, (t, end) in enumerate(OUT_STEPS):
                sp.wait_ge(out_added, c + 1)
                for a, b in CUTS:
                    sp.dma_start(out_v[a:b, t * F:end * F], x_sb[a:b, t * F:end * F]).then_inc(out_stored, 16)
            sp.wait_ge(out_stored, 32 * len(OUT_STEPS))

        @block.gpsimd
        def _(pool):
            nc.gpsimd.memset(ident[:], 0.0).then_inc(pool_const, 1)
            pool.wait_ge(pool_const, 1)
            nc.gpsimd.affine_select(out=ident[:], in_=ident[:], compare_op=ALU.not_equal, fill=1.0, base=0,
                                    pattern=[[-1, P]], channel_multiplier=1).then_inc(pool_const, 1)
            nc.gpsimd.memset(w_node[:], 0.0)
            nc.gpsimd.memset(w_edge[:], 0.0).then_inc(zeroed, 1)
            pool.wait_ge(zeroed, 1)
            for blk in range(2):
                for k, w in enumerate((WK, WV, WQ)):
                    pool.dma_start(w_node[blk * F:(blk + 1) * F, blk, k * F:(k + 1) * F], w).then_inc(weights_loaded, 16)

            def scale(c, s, slot_used):
                pool.wait_ge(rstd_done, c + 1)
                if slot_used:
                    pool.wait_ge(hT_done, c - 1)
                nc.gpsimd.tensor_tensor(
                    h_sb[s].rearrange("p (t f) -> p t f", f=F), centred[:, bass.ds(c * CF, CF)].rearrange("p (t f) -> p t f", f=F),
                    rstd[:, bass.ds(c * CT, CT)][:, :, None].to_broadcast([NP, CT, F]), ALU.mult).then_inc(h_done, 1)

            scale(0, 0, False)
            nc.gpsimd.iota(win_i[:, :], pattern=[[WINDOW, NWINDOW]], base=0, channel_multiplier=0)
            nc.gpsimd.iota(iota_i[:, :], pattern=[[1, WINDOW]], base=0, channel_multiplier=0)
            nc.gpsimd.memset(zeros[:], 0.0)
            nc.gpsimd.memset(q_win[0][:], 0.0)
            nc.gpsimd.memset(q_win[1][:], 0.0)
            nc.gpsimd.memset(src_idx[:, NGROUP:, :], 0).then_inc(pool_const, 1)
            pool.wait_ge(pool_const, 3)
            nc.gpsimd.tensor_copy(win_start[:, :], win_i[:, :])
            nc.gpsimd.tensor_copy(iota_w[:, :], iota_i[:, :]).then_inc(pool_const, 1)
            pool.dma_start(q_table[N:N + WINDOW, :], zeros[:, :]).then_inc(pad_stored, 16)

            scale(1, 1, False)
            with pool.Fori(1, NCHUNK // 2) as i:
                part = bass.ds(i - 1, 1)
                scale(2 * i, 0, True)
                pool.wait_ge(dst_loaded, 48)
                nc.gpsimd.tensor_copy(dst_f[:, part, :], dst_rows[:, part, :]).then_inc(dst_cast, 1)
                scale(2 * i + 1, 1, True)
                pool.wait_ge(dst_cast, i)
                nc.gpsimd.tensor_tensor(rel_rows[:, part, :], dst_f[:, part, :], dst_f[:, part, 0:1].to_broadcast([GP, 1, GROUP]),
                                        ALU.subtract).then_inc(rel_cast, 1)

            def gather(sup, k, slot_used):
                pool.wait_ge(idx_staged, sup + 1)
                if slot_used:
                    pool.wait_ge(msg_done, sup + 1 - UNROLL)
                pool.sem_inc(gather_begun, 1)
                for t in range(TILES):
                    pool.indirect_dma_start(kv[k][:, t, :], None, kv_table,
                                            bass.IndirectOffsetOnAxis(idx_slot[k][:, t:t + 1], 0)).then_inc(kv_gathered[k], 16)

            for s in range(2):
                pool.wait_ge(kv_stored[s], 32 * (NCHUNK // 2))
            for k in range(UNROLL):
                gather(k, k, False)
            with pool.If(any_outside(pool) < 1):
                pool.wait_ge(h_again, NCHUNK)
                for k in range(EARLY):
                    gather(UNROLL + k, UNROLL + k, False)
                for k in range(EARLY, UNROLL):
                    gather(UNROLL + k, k, True)
                with pool.Fori(2, NITER) as i:
                    for k in range(UNROLL):
                        gather(UNROLL * i + k, k, True)
            with pool.Else():
                pool.wait_ge(q_stored[0], 32 * (NCHUNK // 2))
                pool.wait_ge(q_stored[1], 32 * (NCHUNK // 2))
                for k in range(UNROLL):
                    pool.wait_ge(kv_gathered[k], 16 * TILES)
                with pool.Fori(0, NSUPER) as sup:
                    pool.wait_ge(dst_staged, sup + 1)
                    pool.sem_inc(gather_begun, 1)
                    for t in range(TILES):
                        pool.indirect_dma_start(kv[0][:, t, :], None, kv_table,
                                                bass.IndirectOffsetOnAxis(idx_slot[0][:, t:t + 1], 0)).then_inc(kv_gathered[0], 16)
                        pool.indirect_dma_start(q_rows[:, t, :], None, q_table,
                                                bass.IndirectOffsetOnAxis(q_idx[:, t:t + 1], 0)).then_inc(q_gathered, 16)

        @block.scalar
        def _(act):
            for k, b in enumerate((bK, bV, bQ, bE)):
                act.dma_start(b_all[:, k * F:(k + 1) * F], b.rearrange("(o f) -> o f", o=1).to_broadcast([3, F])).then_inc(bias_loaded, 16)
            act.wait_ge(dve_const, 1)
            nc.scalar.activation(zero_col[:], eps_col[:], ACT.Sqrt).then_inc(table_warm, 1)

            def square(c, s, slot_used):
                act.wait_ge(centred_done, c + 1)
                if slot_used:
                    act.wait_ge(sq_summed, c - 1)
                nc.scalar.activation(squared[s][:], centred[:, bass.ds(c * CF, CF)], ACT.Square).then_inc(squared_done, 1)

            def root(c):
                act.wait_ge(sq_summed, c + 1)
                cols = bass.ds(c * CT, CT)
                nc.scalar.activation(std[:, cols], sq_sum[:, cols], ACT.Sqrt, scale=1.0 / F, bias=eps_col[0:NP, :]).then_inc(std_done, 1)

            def keep_hT(n, s, slot_used):
                act.wait_ge(hT_done, n + 1)
                if slot_used:
                    act.wait_ge(rows_done, PAIRS * (n - 1))
                nc.scalar.activation(hT_sb[:, s, :, :], hT_ps[:, :, 0:NP], ACT.Relu).then_inc(hT_copied, 1)

            def keep_rows(n, s, rows_out, stored, stores):
                if stores is not None:
                    act.wait_ge(stored[s], 32 * stores)
                width = rows_out.shape[3]
                for a in range(PAIRS):
                    act.wait_ge(rows_done, PAIRS * n + a + 1)
                    nc.scalar.copy(rows_out[:, s, 2 * a:2 * a + 2, :].rearrange("p t f -> p (t f)"),
                                   node_ps[a][0:NP, 0:2 * width]).then_inc(rows_copied, 1)

            def keep_kv(c, s, stores):
                keep_rows(c, s, kv_out, kv_stored, stores)

            def keep_q(c, s, stores):
                keep_rows(NCHUNK + c, s, q_out, q_stored, stores)

            square(0, 0, False)
            square(1, 1, False)
            root(0)
            root(1)
            keep_hT(0, 0, False)
            square(2, 0, True)
            square(3, 1, True)
            root(2)
            keep_hT(1, 1, False)
            square(4, 0, True)
            root(3)
            keep_kv(0, 0, None)
            keep_hT(2, 0, True)
            square(5, 1, True)
            root(4)
            keep_kv(1, 1, None)
            with act.Fori(3, NCHUNK // 2) as i:
                for s in range(2):
                    c = 2 * i + s
                    square(c, s, True)
                    root(c - 1)
                    keep_hT(c - 3, 1 - s, True)
                    keep_kv(c - 4, s, i - 2)
            root(NCHUNK - 1)
            for c in range(NCHUNK - 4, NCHUNK):
                if c < NCHUNK - 1:
                    keep_hT(c + 1, (c + 1) % 2, True)
                keep_kv(c, c % 2, c // 2)

            nc.scalar.mul(zero_col[:], eps_col[:], 0.0).then_inc(table_warm, 1)
            act.wait_ge(table_warm, 2)
            nc.scalar.copy(acc[:, 5 * RW:], zero_col[:].to_broadcast([P, N + WINDOW - 5 * RW])).then_inc(acc_zeroed, 1)
            nc.scalar.activation(warm_col[:], eps_col[:], ACT.Exp).then_inc(table_warm, 1)
            act.wait_ge(idx_turned, GQ)
            nc.scalar.copy(acc[:, 3 * RW:4 * RW], zero_col[:].to_broadcast([P, RW])).then_inc(acc_zeroed, 1)


            keep_hT(NCHUNK, 0, True)
            for c in range(2):
                keep_hT(NCHUNK + c + 1, 1 - c, True)
                keep_q(c, c, None)
            with act.Fori(1, NCHUNK // 2 - 1) as i:
                for s in range(2):
                    keep_hT(NCHUNK + 2 * i + s + 1, 1 - s, True)
                    keep_q(2 * i + s, s, i)
            keep_hT(2 * NCHUNK - 1, 1, True)
            keep_q(NCHUNK - 2, 0, NCHUNK // 2 - 1)
            keep_q(NCHUNK - 1, 1, NCHUNK // 2 - 1)

            def turned(sup, k, slot_used):
                act.wait_ge(attrT_done, sup + 1)
                if slot_used:
                    act.wait_ge(e_done, sup - 1)
                nc.scalar.copy(attrT[k % 2][:], attrT_ps).then_inc(attrT_copied, 1)
                act.wait_ge(onehotT_done, sup + 1)
                if slot_used:
                    act.wait_ge(qe_done, sup - 1)
                nc.scalar.copy(onehotT[k % 2][:], onehotT_ps).then_inc(onehotT_copied, 1)

            def weights(sup, first):
                act.wait_ge(clip_done, sup + 1)
                if not first:
                    act.wait_ge(msg_done, sup)
                nc.scalar.activation(weight[:], clipped[:], ACT.Exp).then_inc(weight_done, 1)

            with act.If(any_outside(act) < 1):
                for k in range(UNROLL):
                    turned(k, k, k >= 2)
                    if k > 0:
                        weights(k - 1, k == 1)
                with act.Fori(1, NITER) as i:
                    for k in range(UNROLL):
                        turned(UNROLL * i + k, k, True)
                        weights(UNROLL * i + k - 1, False)
                weights(NSUPER - 1, False)
            with act.Else():
                with act.Fori(0, NSUPER) as sup:
                    act.wait_ge(attrT_done, sup + 1)
                    nc.scalar.copy(attrT[0][:], attrT_ps).then_inc(attrT_copied, 1)
                    act.wait_ge(clip_done, sup + 1)
                    nc.scalar.activation(weight[:], clipped[:], ACT.Exp).then_inc(weight_done, 1)

        @block.vector
        def _(dve):
            nc.vector.memset(eps_col[:], EPS).then_inc(dve_const, 1)
            nc.vector.memset(ones3[:], 1.0).then_inc(dve_const, 1)
            nc.vector.memset(ones_col[:], 1.0).then_inc(dve_const, 1)
            def split(n, ins):
                ins.then_inc(split_step, 1)
                dve.wait_ge(split_step, n)

            def split_biases():
                dve.wait_ge(bias_loaded, 64)
                dve.wait_ge(pool_const, 2)
                split(1, nc.vector.tensor_copy(b_part[0][:], b_all[:]))
                split(2, nc.vector.tensor_tensor(b_rest[:], b_all[:], b_part[0][:], ALU.subtract))
                split(3, nc.vector.tensor_copy(b_part[1][:], b_rest[:]))
                split(4, nc.vector.tensor_tensor(b_part[2][:], b_rest[:], b_part[1][:], ALU.subtract))
                split(5, nc.vector.tensor_scalar(b3[:], b_part[0][:], ident[0:3, 0:1], None, ALU.mult))
                split(6, nc.vector.scalar_tensor_tensor(out=b_pick[:], in0=b_part[1][:], scalar=ident[0:3, 1:2], in1=b3[:],
                                                        op0=ALU.mult, op1=ALU.add))
                nc.vector.scalar_tensor_tensor(out=b3[:], in0=b_part[2][:], scalar=ident[0:3, 2:3], in1=b_pick[:],
                                               op0=ALU.mult, op1=ALU.add).then_inc(bias_split, 1)

            def rows_of(a, c):
                return a[:, bass.ds(c * CF, CF)].rearrange("p (t f) -> p t f", f=F)

            def centre(c):
                cols = bass.ds(c * CT, CT)
                nc.vector.tensor_reduce(row_sum[:, cols], rows_of(x_sb, c), AX.X, ALU.add).then_inc(summed, 1)
                dve.wait_ge(summed, c + 1)
                nc.vector.scalar_tensor_tensor(
                    out=rows_of(centred, c), in0=row_sum[:, cols][:, :, None].to_broadcast([NP, CT, F]), scalar=-1.0 / F,
                    in1=rows_of(x_sb, c), op0=ALU.mult, op1=ALU.add).then_inc(centred_done, 1)

            def sum_squares(c, s):
                dve.wait_ge(squared_done, c + 1)
                nc.vector.tensor_reduce(sq_sum[:, bass.ds(c * CT, CT)], squared[s].rearrange("p (t f) -> p t f", f=F),
                                        AX.X, ALU.add).then_inc(sq_summed, 1)

            def invert(c):
                cols = bass.ds(c * CT, CT)
                dve.wait_ge(std_done, c + 1)
                nc.vector.reciprocal(rstd[:, cols], std[:, cols]).then_inc(rstd_done, 1)

            def scale_again(c, s):
                dve.wait_ge(hT_done, NCHUNK + c - 1)
                nc.vector.tensor_tensor(h_sb[s].rearrange("p (t f) -> p t f", f=F), rows_of(centred, c),
                                        rstd[:, bass.ds(c * CT, CT)][:, :, None].to_broadcast([NP, CT, F]), ALU.mult).then_inc(h_again, 1)

            dve.wait_ge(x_loaded[0], 32)
            centre(0)
            centre(1)
            for c in range(2):
                sum_squares(c, c)
                invert(c)
            split_biases()
            dve.wait_ge(x_loaded[1], 32)
            centre(2)
            centre(3)
            sum_squares(2, 0)
            invert(2)
            dve.wait_ge(x_loaded[2], 32)
            centre(4)
            sum_squares(3, 1)
            invert(3)
            centre(5)
            sum_squares(4, 0)
            dve.wait_ge(x_loaded[3], 32)
            with dve.Fori(3, NCHUNK // 2) as i:
                for s in range(2):
                    c = 2 * i + s
                    centre(c)
                    sum_squares(c - 1, 1 - s)
                    invert(c - 2)
            sum_squares(NCHUNK - 1, 1)
            invert(NCHUNK - 2)
            invert(NCHUNK - 1)

            dve.wait_ge(src_loaded, 48)
            nc.vector.tensor_copy(src_f, src_rows).then_inc(src_cast, 1)
            dve.wait_ge(src_cast, 1)
            dve.wait_ge(dst_cast, GQ)
            nc.vector.memset(acc[:, 0:2 * RW], 0.0).then_inc(acc_zeroed, 1)
            dve.wait_ge(rel_cast, GQ)
            nc.vector.memset(acc[:, 2 * RW:3 * RW], 0.0).then_inc(acc_zeroed, 1)
            dve.wait_ge(rstd_done, NCHUNK)
            for s in range(2):
                scale_again(s, s)

            def keep_index(kept, turn, q):
                dve.wait_ge(idx_turned, turn + 1)
                nc.vector.tensor_copy(kept[:, q * GP:(q + 1) * GP, :].rearrange("p r g -> p g r"),
                                      idx_ps[turn % 2][:, 0:G * GP].rearrange("p (g r) -> p g r", g=G)).then_inc(idx_kept, 1)

            def stage_idx(sup, k):
                nc.vector.tensor_copy(idx_slot[k][:].rearrange("p (g h) -> p h g", g=G),
                                      src_idx[:, bass.ds(HALVES * sup, HALVES), :]).then_inc(idx_staged, 1)

            for q in range(GQ):
                keep_index(src_idx, q, q)
            dve.wait_ge(pool_const, 4)
            dve.wait_ge(idx_kept, GQ)
            for k in range(UNROLL + EARLY):
                stage_idx(k, k)
            for q in range(GQ):
                keep_index(dst_rel, GQ + q, q)
            dve.wait_ge(idx_kept, 2 * GQ)
            nc.vector.memset(acc[:, 4 * RW:5 * RW], 0.0).then_inc(acc_zeroed, 1)
            with dve.Fori(1, NCHUNK // 2) as i:
                part = dst_rel[:, bass.ds((i - 1) * GP, GP), :].rearrange("p j g -> p (j g)")
                for s, (found, op) in enumerate(((lows, ALU.min), (highs, ALU.max))):
                    scale_again(2 * i + s, s)
                    nc.vector.tensor_reduce(found[:, bass.ds(i - 1, 1)], part, AX.X, op).then_inc(part_bounded, 1)
            dve.wait_ge(part_bounded, 2 * GQ)
            nc.vector.tensor_reduce(lowest[:], lows[:], AX.X, ALU.min).then_inc(bounds_found, 1)
            nc.vector.tensor_reduce(highest[:], highs[:], AX.X, ALU.max).then_inc(bounds_found, 1)
            dve.wait_ge(bounds_found, 2)
            nc.vector.tensor_scalar(highest[:], highest[:], float(WINDOW), None, ALU.is_ge).then_inc(bounds_found, 1)
            dve.wait_ge(bounds_found, 3)
            nc.vector.scalar_tensor_tensor(out=outside[:], in0=lowest[:], scalar=0.0, in1=highest[:],
                                           op0=ALU.is_lt, op1=ALU.add).then_inc(outside_found, 1)
            nc.vector.memset(dst_rel[0:OVERLAP // G, FULL, :], -1.0).then_inc(masked, 1)
            dve.wait_ge(masked, 1)
            dve.wait_ge(acc_zeroed, 5)

            def build_onehot(sup, k, slot_used):
                if slot_used:
                    dve.wait_ge(sums_done, sup - UNROLL + 1)
                nc.vector.tensor_tensor(
                    onehot[k][:],
                    iota_w[:, None, None, :].to_broadcast([P, G, HALVES, WINDOW]),
                    dst_rel[:, bass.ds(HALVES * sup, HALVES), :].rearrange("p h g -> p g h")[:, :, :, None].to_broadcast([P, G, HALVES, WINDOW]),
                    ALU.is_equal).then_inc(onehot_built, 1)

            def messages(sup, rounds, k, s, restage):
                dve.wait_ge(kv_gathered[k], 16 * TILES * rounds)
                if restage is not None:
                    stage_idx(sup + UNROLL, restage)
                dve.wait_ge(e_done, sup + 1)
                nc.vector.tensor_tensor(prod[:], kv[k][:, :, 0:F], e_ps[s].rearrange("p (t f) -> p t f", f=F),
                                        ALU.mult).then_inc(ke_done, 1)
                dve.wait_ge(qe_done, sup + 1)
                weigh(sup, kv[k], qe_ps[s][:], msg[s])

            def weigh(sup, rows, q, messages_out):
                dve.wait_ge(ke_done, sup + 1)
                nc.vector.scalar_tensor_tensor(
                    out=prod[:].rearrange("p t f -> p (t f)"), in0=prod[:].rearrange("p t f -> p (t f)"),
                    scalar=INV_SQRT_D, in1=q, op0=ALU.mult, op1=ALU.mult).then_inc(keq_done, 1)
                dve.wait_ge(keq_done, sup + 1)
                nc.vector.tensor_reduce(logits[:], prod[:].rearrange("p t (h d) -> p t h d", d=D), AX.X, ALU.add).then_inc(logits_done, 1)
                dve.wait_ge(logits_done, sup + 1)
                nc.vector.tensor_scalar(clipped[:], logits[:], CLIP, -CLIP, ALU.min, ALU.max).then_inc(clip_done, 1)
                dve.wait_ge(weight_done, sup + 1)
                nc.vector.tensor_tensor(
                    messages_out.rearrange("p g h (a d) -> p (g h) a d", d=D),
                    rows[:, :, F:].rearrange("p t (a d) -> p t a d", d=D),
                    weight[:, :, :, None].to_broadcast([P, TILES, H, D]), ALU.mult).then_inc(msg_done, 1)

            def window_starts(sup):
                return [dve.value_load(base_i[0:1, bass.ds(HALVES * sup + h, 1)], min_val=0, max_val=N - 1) for h in range(HALVES)]

            def add_sums(sup, first, base=None):
                base = base or window_starts(sup)
                dve.wait_ge(sums_done, sup + 1)
                for half in range(HALVES):
                    if not first or half:
                        dve.wait_ge(added, HALVES * sup + half)
                    win = acc[0:F, bass.ds(base[half], WINDOW)]
                    nc.vector.tensor_tensor(win, win, sum_ps[0:F, half * WINDOW:(half + 1) * WINDOW], ALU.add).then_inc(added, 1)

            dve.wait_ge(base_loaded, 32)
            dve.wait_ge(outside_counted, 1)
            nc.vector.tensor_copy(scattered[:], base_ps[0:1, 0:1]).then_inc(form_known, 1)
            with dve.If(any_outside(dve) < 1):
                for k in range(2 * UNROLL):
                    build_onehot(k, k % UNROLL, k >= UNROLL)
                    if 0 < k <= UNROLL:
                        early_next = k - 1 < EARLY
                        messages(k - 1, 1, k - 1, (k - 1) % 2, None if early_next else k - 1)
                    elif k > UNROLL:
                        messages(k - 1, 1, k - 1, (k - 1) % 2, k - 1 - UNROLL)
                    if k > 1:
                        add_sums(k - 2, k == 2)
                with dve.Fori(2, NITER) as i:
                    for k in range(UNROLL):
                        sup = UNROLL * i + k
                        build_onehot(sup, k, True)
                        before = (k - 1) % UNROLL
                        messages(sup - 1, i, before, before % 2, before)
                        add_sums(sup - 2, False)
                add_sums(NSUPER - 2, False)
                base = window_starts(NSUPER - 1)
                messages(NSUPER - 1, NITER, UNROLL - 1, (UNROLL - 1) % 2, UNROLL - 1)
                add_sums(NSUPER - 1, False, base)
                dve.wait_ge(added, HALVES * NSUPER)
                dve.sem_inc(edges_summed, 1)
            with dve.Else():
                nc.vector.tensor_copy(base_f[:], base_i[:]).then_inc(base_cast, 1)
                nc.vector.memset(ones_row[:], 1.0).then_inc(base_cast, 1)
                dve.wait_ge(base_spread, 1)
                nc.vector.tensor_tensor(dst_rel[:], dst_rel[:], base_ps[:, 0:NGROUP, None].to_broadcast([P, NGROUP, G]),
                                        ALU.add).then_inc(dst_restored, 1)
                dve.wait_ge(dst_restored, 1)
                nc.vector.memset(dst_rel[0:OVERLAP // G, FULL, :], -1.0).then_inc(dst_restored, 1)
                dve.wait_ge(dst_restored, 2)
                for k in range(UNROLL):
                    dve.wait_ge(kv_gathered[k], 16 * TILES)
                with dve.Fori(0, NSUPER) as sup:
                    nc.vector.tensor_copy(idx_slot[0][:].rearrange("p (g h) -> p h g", g=G), src_idx[:, bass.ds(HALVES * sup, HALVES), :])
                    nc.vector.tensor_copy(dst_now[:].rearrange("p (g h) -> p h g", g=G), dst_rel[:, bass.ds(HALVES * sup, HALVES), :])
                    nc.vector.tensor_scalar(q_idx[:].rearrange("p (g h) -> p h g", g=G), dst_rel[:, bass.ds(HALVES * sup, HALVES), :],
                                            0.0, None, ALU.max).then_inc(dst_staged, 1)
                    dve.wait_ge(kv_gathered[0], 16 * TILES * (sup + 2))
                    dve.wait_ge(q_gathered, 16 * TILES * (sup + 1))
                    dve.wait_ge(e_done, sup + 1)
                    nc.vector.tensor_tensor(prod[:], kv[0][:, :, 0:F], e_ps[0].rearrange("p (t f) -> p t f", f=F),
                                            ALU.mult).then_inc(ke_done, 1)
                    weigh(sup, kv[0], q_rows.rearrange("p t f -> p (t f)"), msg[0])
                    with dve.Fori(0, NWINDOW) as w:
                        turn = sup * NWINDOW + w
                        nc.vector.scalar_tensor_tensor(
                            out=onehot[0].rearrange("p g h w -> p (g h) w"),
                            in0=dst_now[:, :, None].to_broadcast([P, TILES, WINDOW]), scalar=win_start[:, bass.ds(w, 1)],
                            in1=iota_w[:, None, :].to_broadcast([P, TILES, WINDOW]),
                            op0=ALU.subtract, op1=ALU.is_equal).then_inc(onehot_built, 1)
                        dve.wait_ge(sums_done, turn + 1)
                        win = acc[0:F, bass.ds(w * WINDOW, WINDOW)]
                        nc.vector.tensor_tensor(win, win, sum_ps[0:F, 0:WINDOW], ALU.add).then_inc(added, 1)
                        dve.wait_ge(added, turn + 1)
                dve.sem_inc(edges_summed, 1)

            for c, (t, end) in enumerate(OUT_STEPS):
                dve.wait_ge(out_turned, c + 1)
                rows = x_sb[:, t * F:end * F]
                nc.vector.tensor_tensor(rows, rows, wide[c % 2][0:NP, 0:(end - t) * F], ALU.add).then_inc(out_added, 1)

        @block.tensor
        def _(pe):
            pe.wait_ge(pool_const, 2)
            pe.wait_ge(dve_const, 3)

            def turn_h(n, s, bank_used):
                if bank_used:
                    pe.wait_ge(hT_copied, n)
                for a in range(PAIRS):
                    last = nc.tensor.transpose(hT_ps[:, a, 0:NP], h_sb[s][:, 2 * a * F:2 * (a + 1) * F], ident[0:NP, 0:NP])
                last.then_inc(hT_done, 1)

            def project_h(n, s, banks_used, cols, pairs=range(PAIRS)):
                pe.wait_ge(hT_copied, n + 1)
                width = cols.stop - cols.start
                for a in pairs:
                    if banks_used:
                        pe.wait_ge(rows_copied, PAIRS * (n - 1) + a + 1)
                    rows = node_ps[a][0:NP, 0:2 * width]
                    nc.tensor.matmul(rows, ones3[:, 0:NP], b3[:, None, cols].to_broadcast([3, 2, width]), start=True, stop=False)
                    nc.tensor.matmul(rows, hT_sb[:, s, a, :], w_node[:, :, cols], start=False, stop=True).then_inc(rows_done, 1)

            kv_cols, q_cols = slice(0, 2 * F), slice(2 * F, 3 * F)
            pe.wait_ge(h_done, 1)
            turn_h(0, 0, False)
            pe.wait_ge(weights_loaded, 16 * 6)
            pe.wait_ge(bias_split, 1)
            project_h(0, 0, False, kv_cols, range(0, 3))
            pe.wait_ge(h_done, 2)
            turn_h(1, 1, True)
            project_h(0, 0, False, kv_cols, range(3, PAIRS))
            with pe.Fori(1, NCHUNK // 2) as i:
                for s in range(2):
                    c = 2 * i + s
                    pe.wait_ge(h_done, c + 1)
                    turn_h(c, s, True)
                    project_h(c - 1, 1 - s, True, kv_cols)
            project_h(NCHUNK - 1, 1, True, kv_cols)

            def turn_index(rows, first_turn):
                for q in range(GQ):
                    turn = first_turn + q
                    if turn >= 2:
                        pe.wait_ge(idx_kept, turn - 1)
                    for g in range(G):
                        last = nc.tensor.transpose(idx_ps[turn % 2][:, g * GP:(g + 1) * GP],
                                                   rows[:, q, :].rearrange("r (p g) -> r g p", g=G)[:, g, :], ident[0:GP, 0:GP])
                    last.then_inc(idx_turned, 1)

            pe.wait_ge(src_cast, 1)
            turn_index(src_f, 0)
            pe.wait_ge(rel_cast, GQ)
            turn_index(rel_rows, GQ)

            pe.wait_ge(idx_kept, 2 * GQ)
            pe.wait_ge(h_again, 1)
            turn_h(NCHUNK, 0, True)
            pe.wait_ge(h_again, 2)
            turn_h(NCHUNK + 1, 1, True)
            project_h(NCHUNK, 0, True, q_cols)
            with pe.Fori(1, NCHUNK // 2) as i:
                for s in range(2):
                    c = 2 * i + s
                    pe.wait_ge(h_again, c + 1)
                    turn_h(NCHUNK + c, s, True)
                    project_h(NCHUNK + c - 1, 1 - s, True, q_cols)
            project_h(2 * NCHUNK - 1, 1, True, q_cols)

            pe.wait_ge(outside_found, 1)
            pe.wait_ge(idx_kept, 2 * GQ)
            nc.tensor.matmul(base_ps[0:1, 0:1], outside[:], ones_col[:], start=True, stop=True).then_inc(outside_counted, 1)
            pe.wait_ge(rows_copied, 2 * PAIRS * NCHUNK)
            pe.wait_ge(edge_weights_loaded, 32)

            def turn_features(s):
                for g in range(G):
                    last = nc.tensor.transpose(attrT_ps[:, g, :], attr[s].rearrange("p h g f -> p (h g f)")[:, 2 * g * F:2 * (g + 1) * F], ident[:])
                last.then_inc(attrT_done, 1)

            def project_features(s):
                nc.tensor.matmul(e_ps[s][:], ones3[:, :], b3[:, None, 3 * F:].to_broadcast([3, TILES, F]), start=True, stop=False)
                for a in range(G):
                    half, pair = a // 2, a % 2
                    last = nc.tensor.matmul(
                        e_ps[s].rearrange("p (g h f) -> p h g f", g=G, h=HALVES)[:, half, 2 * pair:2 * pair + 2, :],
                        attrT[s][:, a, :], w_edge[:], start=False, stop=a == G - 1)
                last.then_inc(e_done, 1)

            def sum_by_node(messages, hot, apart):
                for half in range(HALVES):
                    block = half if apart else 0
                    for g in range(G):
                        last = nc.tensor.matmul(sum_ps[0:F, block * WINDOW:(block + 1) * WINDOW], messages[:, g, half, :], hot[:, g, half, :],
                                                start=g == 0 and (apart or half == 0), stop=g == G - 1 and (apart or half == HALVES - 1))
                last.then_inc(sums_done, 1)

            def expand(i, k, first):
                sup = UNROLL * i + k
                s = k % 2
                pe.wait_ge(attr_loaded[s], 16 * (UNROLL // 2 * i + k // 2 + 1))
                if not first or k > 0:
                    pe.wait_ge(attrT_copied, sup)
                turn_features(s)
                pe.wait_ge(onehot_built, sup + 1)
                if not first or k > 0:
                    pe.wait_ge(onehotT_copied, sup)
                for g in range(G):
                    last = nc.tensor.transpose(onehotT_ps[:, g, :], onehot[k][:, g, :, :].rearrange("p h w -> p (h w)"), ident[:])
                last.then_inc(onehotT_done, 1)
                pe.wait_ge(attrT_copied, sup + 1)
                if not first or k >= 2:
                    pe.wait_ge(ke_done, sup - 1)
                project_features(s)
                pe.wait_ge(onehotT_copied, sup + 1)
                pe.wait_ge(q_loaded[s], 32 * (UNROLL // 2 * i + k // 2 + 1))
                if not first or k >= 2:
                    pe.wait_ge(keq_done, sup - 1)
                for g in range(G):
                    last = nc.tensor.matmul(qe_ps[s][:, 2 * g * F:2 * (g + 1) * F],
                                            onehotT[s][:, g, :], q_win[s].rearrange("k h f -> k (h f)"), start=True, stop=True)
                last.then_inc(qe_done, 1)

            def sum_messages(sup, k, first):
                pe.wait_ge(msg_done, sup + 1)
                if not first:
                    pe.wait_ge(added, HALVES * sup)
                sum_by_node(msg[k % 2], onehot[k], True)

            with pe.If(any_outside(pe) < 1):
                for k in range(UNROLL):
                    expand(0, k, True)
                    if k > 0:
                        sum_messages(k - 1, k - 1, k == 1)
                with pe.Fori(1, NITER) as i:
                    for k in range(UNROLL):
                        expand(i, k, False)
                        sum_messages(UNROLL * i + k - 1, (k - 1) % UNROLL, False)
                sum_messages(NSUPER - 1, UNROLL - 1, False)
            with pe.Else():
                pe.wait_ge(base_cast, 2)
                nc.tensor.matmul(base_ps[:, 0:NGROUP], ones_row[:], base_f[:], start=True, stop=True).then_inc(base_spread, 1)
                with pe.Fori(0, NSUPER) as sup:
                    pe.wait_ge(attr_loaded[0], 16 * (sup + 1))
                    turn_features(0)
                    pe.wait_ge(attrT_copied, sup + 1)
                    pe.wait_ge(dst_staged, sup + 1)
                    project_features(0)
                    with pe.Fori(0, NWINDOW) as w:
                        pe.wait_ge(msg_done, sup + 1)
                        pe.wait_ge(onehot_built, sup * NWINDOW + w + 1)
                        sum_by_node(msg[0], onehot[0], False)

            pe.wait_ge(edges_summed, 1)
            acc_nodes = acc[0:F, 0:N].rearrange("p (n t) -> p t n", t=NPP)
            for c, (t, end) in enumerate(OUT_STEPS):
                if c >= 2:
                    pe.wait_ge(out_added, c - 1)
                for k in range(end - t):
                    last = nc.tensor.transpose(wide[c % 2][0:NP, k * F:(k + 1) * F], acc_nodes[:, t + k, :], ident[0:F, 0:F])
                last.then_inc(out_turned, 1)


_INS = ["x", "src", "dst", "edge_attr_64", "L0_gnn_WQ", "L0_gnn_bQ", "L0_gnn_WK", "L0_gnn_bK",
        "L0_gnn_WE", "L0_gnn_bE", "L0_gnn_WV", "L0_gnn_bV"]


def kernel(**inputs):
    import concourse.bacc as _bacc
    from concourse.bass_utils import run_bass_kernel_spmd as _run

    nc = _bacc.Bacc("TRN2", target_bir_lowering=False, num_devices=1)
    arrays, args = {}, []
    for name in _INS:
        a = np.ascontiguousarray(inputs[name])
        arrays[f"in_{name}"] = a
        args.append(nc.dram_tensor(f"in_{name}", a.shape, mybir.dt.from_np(a.dtype), kind="ExternalInput").ap())
    out = nc.dram_tensor("out_0", (N, F), FP32, kind="ExternalOutput").ap()
    build(nc, *args, out)
    r = _run(nc, [arrays], core_ids=[0])
    return r.results[0]["out_0"]
```
